# Optimizing a Trainium2 kernel written in Bass

```python
import numpy as np
import jax
import jax.numpy as jnp

def _softmax(x, axis=-1):
    return jax.nn.softmax(x, axis=axis)

def _gelu(x):
    return jax.nn.gelu(x, approximate=True)

def _silu(x):
    return jax.nn.silu(x)

def _sigmoid(x):
    return jax.nn.sigmoid(x)

def _layernorm(x, axis=-1, eps=1e-05):
    m = jnp.mean(x, axis=axis, keepdims=True)
    v = jnp.var(x, axis=axis, keepdims=True)
    return (x - m) / jnp.sqrt(v + eps)

def _scatter_add(tgt, idx, src, axis=0):
    return tgt.at[idx].add(src)

def _segment_sum(src, seg, n):
    return jax.ops.segment_sum(src, seg, n)
kernel_name = 'mk_seq_postln_d1_jaxref_r8_97aa34'

def setup_inputs(seed: int=0):
    np.random.seed(seed)
    _w = jnp.asarray

    def _L0_attn_setup():
        import jax, jax.numpy as jnp
        import numpy as np
        D_MODEL = 128
        N_HEADS = 16
        N_GROUPS = 4
        CONTEXT_LEN = 64
        D_H = D_MODEL // N_HEADS
        GROUP_SIZE = N_HEADS // N_GROUPS
        B, S = (4, 256)
        key = jax.random.key(seed)
        ks = jax.random.split(key, 9)
        s = 0.02
        return {'x': jax.random.normal(ks[0], (B, S, D_MODEL), dtype=jnp.float32), 'Wq': jax.random.normal(ks[1], (D_MODEL, D_MODEL), dtype=jnp.float32) * s, 'bq': jax.random.normal(ks[2], (D_MODEL,), dtype=jnp.float32) * s, 'Wk': jax.random.normal(ks[3], (D_MODEL, N_GROUPS * D_H), dtype=jnp.float32) * s, 'bk': jax.random.normal(ks[4], (N_GROUPS * D_H,), dtype=jnp.float32) * s, 'Wv': jax.random.normal(ks[5], (D_MODEL, N_GROUPS * D_H), dtype=jnp.float32) * s, 'bv': jax.random.normal(ks[6], (N_GROUPS * D_H,), dtype=jnp.float32) * s, 'Wo': jax.random.normal(ks[7], (D_MODEL, D_MODEL), dtype=jnp.float32) * s, 'bo': jax.random.normal(ks[8], (D_MODEL,), dtype=jnp.float32) * s}
    _L0_attn_in = _L0_attn_setup()

    def _L0_ffn_setup():
        import jax, jax.numpy as jnp
        import numpy as np
        B, S, D = (2, 256, 128)
        E, H, K = (8, 704, 2)
        N_RESERVED = 4
        key = jax.random.key(seed)
        ks = jax.random.split(key, 5)
        scale = 0.02
        x = jax.random.normal(ks[0], (B, S, D), dtype=jnp.float32)
        gate_w = jax.random.normal(ks[1], (E, D), dtype=jnp.float32) * scale
        w1 = jax.random.normal(ks[2], (E, D, H), dtype=jnp.float32) * scale
        w3 = jax.random.normal(ks[3], (E, D, H), dtype=jnp.float32) * scale
        w2 = jax.random.normal(ks[4], (E, H, D), dtype=jnp.float32) * scale
        return {'x': x, 'gate_w': gate_w, 'w1': w1, 'w2': w2, 'w3': w3}
    _L0_ffn_in = _L0_ffn_setup()
    _d = {'L0_attn_x': _L0_attn_in['x'], 'L0_attn_Wq': _L0_attn_in['Wq'], 'L0_attn_bq': _L0_attn_in['bq'], 'L0_attn_Wk': _L0_attn_in['Wk'], 'L0_attn_bk': _L0_attn_in['bk'], 'L0_attn_Wv': _L0_attn_in['Wv'], 'L0_attn_bv': _L0_attn_in['bv'], 'L0_attn_Wo': _L0_attn_in['Wo'], 'L0_attn_bo': _L0_attn_in['bo'], 'L0_ffn_gate_w': _L0_ffn_in['gate_w'], 'L0_ffn_w1': _L0_ffn_in['w1'], 'L0_ffn_w2': _L0_ffn_in['w2'], 'L0_ffn_w3': _L0_ffn_in['w3']}
    _x0 = _d['L0_attn_x']
    _d['L0_attn_x'] = jax.random.normal(jax.random.fold_in(jax.random.key(seed), 1), (32, 256, 128), dtype=_x0.dtype)
    del _x0
    return _d

def reference(L0_attn_x, L0_attn_Wq, L0_attn_bq, L0_attn_Wk, L0_attn_bk, L0_attn_Wv, L0_attn_bv, L0_attn_Wo, L0_attn_bo, L0_ffn_gate_w, L0_ffn_w1, L0_ffn_w2, L0_ffn_w3):

    def _L0_attn_ref(x, Wq, bq, Wk, bk, Wv, bv, Wo, bo):
        import jax, jax.numpy as jnp
        import numpy as np
        D_MODEL = 128
        N_HEADS = 16
        N_GROUPS = 4
        CONTEXT_LEN = 64
        D_H = D_MODEL // N_HEADS
        GROUP_SIZE = N_HEADS // N_GROUPS
        B, S = (4, 256)
        b, s = (x.shape[0], x.shape[1])
        q = (x @ Wq + bq).reshape(b, s, N_GROUPS, GROUP_SIZE, D_H)
        q = jnp.transpose(q, (0, 2, 3, 1, 4))
        k = jnp.transpose((x @ Wk + bk).reshape(b, s, N_GROUPS, D_H), (0, 2, 1, 3))
        v = jnp.transpose((x @ Wv + bv).reshape(b, s, N_GROUPS, D_H), (0, 2, 1, 3))
        scores = jnp.einsum('bghqd,bgkd->bghqk', q, k) / jnp.sqrt(jnp.float32(D_H))
        i = jnp.arange(s)
        j = jnp.arange(s)
        upper = (i - CONTEXT_LEN)[:, None] >= j[None, :]
        lower = i[:, None] < j[None, :]
        mask = upper | lower
        scores = jnp.where(mask, jnp.float32(-1000000000.0), scores)
        att = jax.nn.softmax(scores, axis=-1)
        out = jnp.einsum('bghqk,bgkd->bghqd', att, v)
        out = jnp.transpose(out, (0, 3, 1, 2, 4)).reshape(b, s, D_MODEL)
        return out @ Wo + bo

    def _L0_ffn_ref(x, gate_w, w1, w2, w3):
        import jax, jax.numpy as jnp
        import numpy as np
        B, S, D = (2, 256, 128)
        E, H, K = (8, 704, 2)
        N_RESERVED = 4
        b, s, d = x.shape
        T = b * s
        xf = x.reshape(T, d)
        logits = xf @ gate_w.T
        expert_ids = jnp.arange(E)
        logits = jnp.where(expert_ids[None, :] >= E - N_RESERVED, -jnp.inf, logits)
        weights = jax.nn.softmax(logits, axis=-1)
        top_w, top_idx = jax.lax.top_k(weights, K)
        top_w = top_w / jnp.sum(top_w, axis=-1, keepdims=True)
        cw = jnp.zeros((T, E), dtype=x.dtype).at[jnp.arange(T)[:, None], top_idx].add(top_w)
        h = jax.nn.silu(jnp.einsum('td,edh->teh', xf, w1)) * jnp.einsum('td,edh->teh', xf, w3)
        y = jnp.einsum('teh,ehd->ted', h, w2)
        out = jnp.einsum('te,ted->td', cw, y)
        return out.reshape(b, s, d)
    x = L0_attn_x
    x = _layernorm(x + _L0_attn_ref(x, L0_attn_Wq, L0_attn_bq, L0_attn_Wk, L0_attn_bk, L0_attn_Wv, L0_attn_bv, L0_attn_Wo, L0_attn_bo), axis=-1)
    x = _layernorm(x + _L0_ffn_ref(x, L0_ffn_gate_w, L0_ffn_w1, L0_ffn_w2, L0_ffn_w3), axis=-1)
    return x

_drawn_inputs = setup_inputs


def setup_inputs(seed=0):
    import zlib

    import numpy as np

    out = dict(_drawn_inputs(seed))
    spreads = {}
    factors = {'L0_attn_Wq': 8.0,
     'L0_attn_bq': 8.0,
     'L0_attn_Wk': 8.0,
     'L0_attn_bk': 8.0,
     'L0_attn_Wv': 6.273,
     'L0_attn_bv': 8.0,
     'L0_attn_Wo': 5.503,
     'L0_attn_bo': 2.68,
     'L0_ffn_gate_w': 8.0,
     'L0_ffn_w1': 5.851,
     'L0_ffn_w2': 5.824,
     'L0_ffn_w3': 5.818}
    for name, (base, spread) in spreads.items():
        noise = np.random.default_rng([zlib.crc32(name.encode()), seed]).standard_normal(out[name].shape)
        drawn = base * np.exp(spread * noise) if base else spread * noise
        out[name] = jnp.asarray(drawn.astype(out[name].dtype))
    for name, factor in factors.items():
        out[name] = (out[name] * factor).astype(out[name].dtype)
    return out
```

```python
from contextlib import ExitStack

import concourse.bass as bass
from concourse import mybir

F32 = mybir.dt.float32
F16 = mybir.dt.float16
BF16 = mybir.dt.bfloat16
ALU = mybir.AluOpType
ACT = mybir.ActivationFunctionType
AX = mybir.AxisListType

P = 128
B, S, D = 32, 256, 128
NH, NG, DH = 16, 4, 8
R = NH // NG
W = 64
UB = S // W
KW = 2 * W
HB = S // P
NBLK = B * HB
SLOTS = 4
VC = 2 * DH + 1
E, EA, TOPK = 8, 4, 2
H = 704
HC = H // P
HT = H - HC * P
WC = 2 * H
W2C = (HC + 1) * D
WALL = EA * (WC + W2C)
WSTEP = WALL // B
TB = 4
TT = TB * P
NGATE, NFIN = 12, 12
NT = NBLK // TB
SCALE = float(DH) ** -0.5
EPS = 1e-5
C_ID, C_MS, C_MS0, C_MT, C_MT0, C_NQ, C_NK, C_N1, C_TRI = 0, 128, 256, 384, 448, 512, 513, 514, 515
C_ALL = C_TRI + EA * EA
assert WALL % B == 0 and HT * 2 == P


def build(nc, x, wq, bq, wk, bk, wv, bv, wo, bo, gate, w1, w2, w3, const, out):
    ctx = ExitStack()
    with ctx:
        def sb(name, shape, dt):
            return ctx.enter_context(nc.sbuf_tensor(name, shape, dt))

        def pb(name, shape, dt=F32):
            return ctx.enter_context(nc.psum_tensor(name, shape, dt))

        def sem(name):
            return ctx.enter_context(nc.semaphore(name))

        xr = sb("xr", [P, NBLK, D], F32)
        stats = sb("stats", [P, NBLK, 6], F32)
        wall32 = sb("wall32", [P, WALL], F32)
        wallh = sb("wallh", [P, WALL], F16)
        walll = sb("walll", [P, WALL], F16)
        cst = sb("cst", [P, C_ALL], F32)
        identb = sb("identb", [P, P], BF16)
        nidentb = sb("nidentb", [P, P], BF16)
        onesh = sb("onesh", [P, S], F16)
        mask_s = sb("mask_s", [P, 2, NG, KW], BF16)
        mask_t = sb("mask_t", [P, 2, 8, W], BF16)
        wqkv32 = sb("wqkv32", [P, D + 2 * NG * DH], F32)
        wqkvh = sb("wqkvh", [P, D + 2 * NG * DH], F16)
        wqkvl = sb("wqkvl", [P, D + 2 * NG * DH], F16)
        wqh = sb("wqh", [P, R, NG, SLOTS, DH], F16)
        wql = sb("wql", [P, R, NG, SLOTS, DH], F16)
        wkh = sb("wkh", [P, NG, SLOTS, DH], F16)
        wkl = sb("wkl", [P, NG, SLOTS, DH], F16)
        wo32 = sb("wo32", [P, 2, D], F32)
        woh = sb("woh", [P, 2, D], F16)
        wol = sb("wol", [P, 2, D], F16)
        bias32 = sb("bias32", [2, 2 * D + 2 * NG * DH], F32)
        biash = sb("biash", [2, 2 * D + 2 * NG * DH], F16)
        biasm = sb("biasm", [2, 2 * D + 2 * NG * DH], F16)
        bqr = sb("bqr", [P, R, NG, SLOTS, DH], F16)
        bkr = sb("bkr", [P, NG, SLOTS, DH], F16)
        bvr = sb("bvr", [P, NG * DH], F16)
        bor = sb("bor", [P, D], F16)
        g32 = sb("g32", [P, EA], F32)
        gh = sb("gh", [P, EA], F16)
        gl = sb("gl", [P, EA], F16)
        xst = sb("xst", [P, HB, D], F32)
        xth = sb("xth", [P, W + S], F16)
        xtl = sb("xtl", [P, W + S], F16)
        qh = sb("qh", [P, R * S], F16)
        qa = sb("qa", [P, 2, UB, R, W], F16)
        kh = sb("kh", [P, S], F16)
        km = sb("km", [P, S], F16)
        kbd = sb("kbd", [P, 2, NG, W + S], F16)
        vaug = sb("vaug", [P, 2, UB, NG, VC], F16)
        mx = sb("mx", [P, 2, 2, NG, 32], BF16)
        qm = sb("qm", [P, 2, R, W], F16)
        p32 = sb("p32", [P, 2, NH * W], F32)
        ph = sb("ph", [P, 4, NH * W], F16)
        pl = sb("pl", [P, 4, NH * W], F16)
        rden = sb("rden", [P, 2 * 8], F32)
        ot2 = sb("ot2", [P, 2 * 8, 2 * DH], F32)
        o32 = sb("o32", [P, 2 * 8, DH], F32)
        oth = sb("oth", [P, P], F16)
        otl = sb("otl", [P, P], F16)
        rs = sb("rs", [P, 6, NBLK], F32)
        rstd = sb("rstd", [P, NBLK], F32)
        nmr = sb("nmr", [P, NBLK], F32)
        x1st = sb("x1st", [P, TB, D], F32)
        x1h = sb("x1h", [P, TT], F16)
        x1l = sb("x1l", [P, TT], F16)
        sg = sb("sg", [P, 3, TT], F32)
        hf = sb("hf", [P, 3, TT], F32)
        nh = (HC + 1) * TT
        hh, hl = (wall32[:, n * nh:(n + 1) * nh].bitcast(F16).rearrange("p (b c t) -> p b c t", b=2, c=HC + 1) for n in range(2))
        lg = sb("lg", [P, TB, EA], F32)
        gt = sb("gt", [P, TB, EA, EA], F32)
        eq = sb("eq", [P, TB, EA, EA], F32)
        rank = sb("rank", [P, TB, EA], F32)
        gm = sb("gm", [P, TB], F32)
        ge = sb("ge", [P, TB, EA], F32)
        ex = sb("ex", [P, TB, EA], F32)
        cwu = sb("cwu", [P, TB, EA], F32)
        gs = sb("gs", [P, TB], F32)
        gr = sb("gr", [P, TB], F32)
        cw = sb("cw", [P, TB, EA], F32)
        fst = sb("fst", [P, TB, 6], F32)
        fs = sb("fs", [P, 6, TB], F32)
        frs = sb("frs", [P, TB], F32)
        fnm = sb("fnm", [P, TB], F32)
        yst = sb("yst", [P, TB, D], F32)
        ost = sb("ost", [P, TB, D], F32)
        bank = [pb(f"bank{i}", [P, 1024]) for i in range(4)]
        ps_s, ps_t = bank[0], bank[1]
        b45, b67 = bank[2], bank[3]
        ps_m = b45[:, 0:R * W]
        ps_o = b45[:, 512:512 + 2 * 8 * VC]
        ps_x, ps_k, ps_v, ps_q = b67[:, 0:S], b67[:, 0:S], b67[:, 512:512 + UB * NG * DH], b67[:, :]

        ld_x = sem("ld_x")
        ld_small = sem("ld_small")
        ld_big = sem("ld_big")
        st_out = sem("st_out")
        setup = sem("setup")
        e_scores, e_maxt, e_tscores, e_pv = sem("e_scores"), sem("e_maxt"), sem("e_tscores"), sem("e_pv")
        e_xt, e_k, e_q, e_v, e_ot, e_op = (sem(n) for n in ("e_xt", "e_k", "e_q", "e_v", "e_ot", "e_op"))
        a_xh, a_kh, a_qh, a_vh, a_oth, a_p32, a_ph, a_w = (
            sem(n) for n in ("a_xh", "a_kh", "a_qh", "a_vh", "a_oth", "a_p32", "a_ph", "a_w"))
        v_xst, v_xl, v_km, v_kbd, v_qa, v_vl, v_mx, v_qm, v_rden, v_o, v_otl, v_r, v_w = (
            sem(n) for n in ("v_xst", "v_xl", "v_km", "v_kbd", "v_qa", "v_vl", "v_mx", "v_qm", "v_rden",
                             "v_o", "v_otl", "v_r", "v_w"))
        g_pl, g_o = sem("g_pl"), sem("g_o")
        v_chain = sem("v_chain")
        v_stats, v_x1n, v_gc, v_fc = (sem(n) for n in ("v_stats", "v_x1n", "v_gc", "v_fc"))
        a_sq = sem("a_sq")
        e_x1, e_gate, e_h, e_y = sem("e_x1"), sem("e_gate"), sem("e_h"), sem("e_y")
        a_x1h, a_silu, a_hh, a_ex, a_fsq = (sem(n) for n in ("a_x1h", "a_silu", "a_hh", "a_ex", "a_fsq"))
        v_x1, v_x1l, v_hf, v_hl, v_y, v_fv, v_out = (
            sem(n) for n in ("v_x1", "v_x1l", "v_hf", "v_hl", "v_y", "v_fv", "v_out"))

        def past(n):
            return max(n, 0) if isinstance(n, int) else n

        block = ctx.enter_context(nc.Block())

        def pairs(eng, body, lo, hi):
            for b in (-1, 0, 1):
                body(b, b % 2)
            with eng.Fori(1, B // 2 - 1) as i:
                for par in range(2):
                    body(i * 2 + par, par)
            for b in (B - 2, B - 1, B):
                body(b, b % 2)

        def has(b, k):
            return not isinstance(b, int) or 0 <= b + k < B

        @block.sync
        def _(sp):
            sp.dma_start(xr[:, 0:HB, :], x[0].rearrange("(h p) d -> p h d", p=P)).then_inc(ld_x, 16)
            sp.dma_start(cst[:, :], const).then_inc(ld_small, 16)
            sp.dma_start(wqkv32[:, 0:D], wq).then_inc(ld_small, 16)
            sp.dma_start(wqkv32[:, D:D + 32], wk).then_inc(ld_small, 16)
            sp.dma_start(wqkv32[:, D + 32:D + 64], wv).then_inc(ld_small, 16)
            for n, (b, w) in enumerate(((bq, D), (bk, 32), (bv, 32), (bo, D))):
                at = (0, D, D + 32, D + 64)[n]
                for row in range(2):
                    sp.dma_start(bias32[row:row + 1, at:at + w], b.rearrange("(a n) -> a n", a=1)).then_inc(ld_small, 16)
            for half in range(2):
                for r1 in range(2):
                    for g in range(NG):
                        for rp in range(2):
                            h0 = (g * R + rp * 2 + r1) * DH
                            p0 = half * 64 + (g * 2 + rp) * DH
                            sp.dma_start(wo32[p0:p0 + DH, r1, :], wo[h0:h0 + DH, :]).then_inc(ld_small, 16)
            sp.dma_start(g32[:, :], gate[0:EA, :].rearrange("e d -> d e"), allow_slow_non_contiguous=True).then_inc(ld_small, 16)
            with sp.Fori(1, B) as b:
                sp.wait_ge(ld_x, b * 16)
                sp.dma_start(xr[:, bass.ds(b * HB, HB), :],
                             x[bass.ds(b, 1)].rearrange("o (h p) d -> p (o h) d", p=P)).then_inc(ld_x, 16)
            with sp.Fori(1, NT + 1) as i:
                sp.wait_ge(v_out, i)
                sp.dma_start(out[bass.ds(i * TB - TB, TB)].rearrange("k p d -> p k d"), ost[:, :, :]).then_inc(st_out, 16)
            sp.wait_ge(st_out, 16 * NT)

        N_SMALL = 1 + 3 + 8 + 32 + 1
        N_BIG = EA * 6

        @block.gpsimd
        def _(pool):
            pool.memset(wall32[64:P, :], 0.0).then_inc(v_w, 1)
            pool.wait_ge(v_w, 1)
            for e in range(EA):
                c = e * WC
                pool.dma_start(wall32[:, c:c + HC * P], w1[e, :, 0:HC * P]).then_inc(ld_big, 16)
                pool.dma_start(wall32[:, c + HC * P:c + 2 * HC * P], w3[e, :, 0:HC * P]).then_inc(ld_big, 16)
                pool.dma_start(wall32[:, c + 2 * HC * P:c + 2 * HC * P + HT], w1[e, :, HC * P:H]).then_inc(ld_big, 16)
                pool.dma_start(wall32[:, c + 2 * HC * P + HT:c + WC], w3[e, :, HC * P:H]).then_inc(ld_big, 16)
                c = EA * WC + e * W2C
                pool.dma_start(wall32[:, c:c + HC * D].rearrange("p (k d) -> p k d", k=HC),
                               w2[e, 0:HC * P, :].rearrange("(k p) d -> p k d", p=P)).then_inc(ld_big, 16)
                pool.dma_start(wall32[0:HT, c + HC * D:c + W2C], w2[e, HC * P:H, :]).then_inc(ld_big, 16)

            def body(b, par):
                def lo_part(t, k):
                    pool.wait_ge(a_ph, t + 1)
                    pool.wait_ge(e_pv, past(t - 3))
                    pool.tensor_tensor(pl[:, k % 4, :], p32[:, k % 2, :], ph[:, k % 4, :], ALU.subtract).then_inc(g_pl, 1)

                def sum_o(n):
                    pool.wait_ge(v_o, n + 1)
                    pool.wait_ge(e_ot, past(n))
                    pool.tensor_tensor(o32[:, :, :], ot2[:, :, 0:DH], ot2[:, :, DH:2 * DH], ALU.add).then_inc(g_o, 1)

                for s in range(UB):
                    if s in (0, 2) and has(b, -1):
                        sum_o(b * HB - HB + s // 2)
                    if has(b, 0):
                        lo_part(b * UB + s, UB * par + s)
            pairs(pool, body, 0, 0)

        @block.tensor
        def _(pe):
            pe.wait_ge(setup, 1)

            def transpose_x(b):
                pe.wait_ge(v_xst, b + 1)
                pe.wait_ge(v_qa, past(b))
                pe.wait_ge(v_vl, past(b))
                for h in range(HB):
                    last = pe.transpose(ps_x[:, h * P:(h + 1) * P], xst[:, h, :], cst[:, C_ID:C_ID + P])
                last.then_inc(e_xt, 1)

            def project_k(b):
                pe.wait_ge(v_xl, b + 1)
                pe.wait_ge(a_xh, b + 1)
                for n, (w, m) in enumerate(((bkr, onesh[:, 0:S]), (wkh, xth[:, W:]), (wkh, xtl[:, W:]), (wkl, xth[:, W:]))):
                    last = pe.matmul(ps_k, w[:, :, :, :].rearrange("p g s d -> p (g s d)"), m, start=n == 0, stop=n == 3)
                last.then_inc(e_k, 1)

            def project_q(b):
                pe.wait_ge(v_km, b + 1)
                for j in range(2):
                    cols = slice(W + j * P, W + (j + 1) * P)
                    for r in range(R):
                        o = ps_q[:, j * 512:(j + 1) * 512].rearrange("p (a r q) -> p a r q", a=2, r=R)[:, :, r, :]
                        for n, (w, m) in enumerate(((bqr, onesh[:, 0:P]), (wqh, xth[:, cols]), (wqh, xtl[:, cols]), (wql, xth[:, cols]))):
                            last = pe.matmul(o, w[:, r, :, :, :].rearrange("p g s d -> p (g s d)"), m, start=n == 0, stop=n == 3)
                last.then_inc(e_q, 1)

            def project_v(b):
                pe.wait_ge(v_qa, b + 1)
                for a in range(UB):
                    o = ps_v[:, a * 32:(a + 1) * 32]
                    win = slice(a * W, a * W + KW)
                    for n, (l, r) in enumerate(((onesh[:, 0:P], bvr[:, :]), (xth[:, win], wqkvh[:, D + 32:]),
                                                (xtl[:, win], wqkvh[:, D + 32:]), (xth[:, win], wqkvl[:, D + 32:]))):
                        last = pe.matmul(o, l, r, start=n == 0, stop=n == 3)
                last.then_inc(e_v, 1)

            def scores(b, par, a):
                t = b * UB + a
                if a == 0:
                    pe.wait_ge(v_qa, b + 1)
                    pe.wait_ge(v_kbd, b + 1)
                pe.wait_ge(v_mx, past(t))
                for rp in range(2):
                    o = ps_s[:, rp * 512:(rp + 1) * 512]
                    pe.matmul(o, identb[:, :], mask_s[:, int(a == 0), :, :].rearrange("p g k -> p (g k)"), start=True, stop=False)
                    last = pe.matmul(o, qa[:, par, a, 2 * rp:2 * rp + 2, :].rearrange("p r q -> p (r q)"),
                                     kbd[:, par, :, a * W:a * W + KW], start=False, stop=True)
                last.then_inc(e_scores, 1)

            def max_rows(t, k):
                pe.wait_ge(v_mx, t + 1)
                pe.wait_ge(v_qm, past(t))
                for rp in range(2):
                    last = pe.matmul(ps_m[:, rp * P:(rp + 1) * P], mx[:, k % 2, rp, :, :].rearrange("p g c -> p (g c)"),
                                     nidentb[:, :], start=True, stop=True)
                last.then_inc(e_maxt, 1)

            def tscores(b, par, a):
                t = b * UB + a
                pe.wait_ge(v_qm, t + 1)
                pe.wait_ge(a_ph, past(t))
                for j in range(2):
                    o = ps_t[:, j * 512:(j + 1) * 512]
                    pe.matmul(o, identb[:, :], mask_t[:, int(a == 0), :, :].rearrange("p h q -> p (h q)"), start=True, stop=False)
                    for g in (2 * j, 2 * j + 1):
                        last = pe.matmul(ps_t[:, g * 256:(g + 1) * 256], kbd[:, par, g, a * W:a * W + KW],
                                         qm[:, a % 2, :, :].rearrange("p r q -> p (r q)"), start=False, stop=g % 2 == 1)
                last.then_inc(e_tscores, 1)

            def pv(b, par, a):
                t = b * UB + a
                pe.wait_ge(g_pl, t + 1)
                pe.wait_ge(a_ph, t + 1)
                pe.wait_ge(v_vl, b + 1)
                pe.wait_ge(v_o, past(b * HB + a // 2))
                k = (UB * par + a) % 4
                for g in range(NG):
                    for rp in range(2):
                        n = (a % 2) * 8 + g * 2 + rp
                        c = (g * 2 + rp) * P
                        pe.matmul(ps_o[:, n * VC:(n + 1) * VC], ph[:, k, c:c + P], vaug[:, par, a, g, :], start=True, stop=False)
                        last = pe.matmul(ps_o[:, n * VC:(n + 1) * VC], pl[:, k, c:c + P], vaug[:, par, a, g, :], start=False, stop=True)
                last.then_inc(e_pv, 1)

            def transpose_o(n):
                pe.wait_ge(g_o, n + 1)
                pe.transpose(ps_m[:, 0:P], o32[:, :, :].rearrange("p a b -> p (a b)"), cst[:, C_ID:C_ID + P]).then_inc(e_ot, 1)

            def project_o(n):
                pe.wait_ge(v_otl, n + 1)
                pe.matmul(ps_m[:, 0:D], onesh[:, 0:P], bor[:, :], start=True, stop=True)
                for m, (l, r) in enumerate(((oth, woh), (otl, woh), (oth, wol))):
                    for r1 in range(2):
                        for u in range(2):
                            rows = slice(u * 64, (u + 1) * 64)
                            last = pe.matmul(ps_m[rows, 0:D], l[rows, r1 * 64:(r1 + 1) * 64], r[rows, r1, :],
                                             start=False, stop=m == 2 and r1 == 1, skip_group_check=True)
                last.then_inc(e_op, 1)

            def body(b, par):
                for a in range(UB):
                    t = b * UB + a
                    k = par * UB + a
                    if a < UB - 1 and has(b, 0):
                        scores(b, par, a + 1)
                    if a == UB - 1 and has(b, 1):
                        scores(b + 1, 1 - par, 0)
                    if has(b, -1):
                        n = b * HB - HB + a // 2
                        if has(b, 0):
                            pe.wait_ge(v_qm, t + 1)
                        if a % 2 == 0:
                            transpose_o(n)
                        else:
                            project_o(n)
                    if has(b, 0):
                        tscores(b, par, a)
                    if a == 0 and has(b, 1):
                        project_k(b + 1)
                    if a == 1 and has(b, 1):
                        project_q(b + 1)
                    if a < 2 and has(b, -1):
                        pv(b - 1, 1 - par, a + 2)
                    if a >= 2 and has(b, 0):
                        pv(b, par, a - 2)
                    if a == 2 and has(b, 1):
                        project_v(b + 1)
                    if a == 3 and has(b, 2):
                        transpose_x(b + 2)
                    if (a < UB - 1 and has(b, 0)) or (a == UB - 1 and has(b, 1)):
                        if has(b, -1):
                            if a % 2 == 0:
                                pe.wait_ge(v_otl, n + 1)
                            else:
                                pe.wait_ge(v_r, n + 1)
                        max_rows(t + 1, k + 1)

            transpose_x(0)
            pairs(pe, body, 0, 0)

            pe.wait_ge(v_w, B + 1)
            ident = cst[:, C_ID:C_ID + P]
            b01, b23, b45_, b67_ = bank

            def hbank(n, which):
                return bank[n % 3][:, which * 512:(which + 1) * 512]

            y = bank[3][:, 0:512]
            xg = bank[3][:, 512:1024]

            def transpose_x1(i):
                pe.wait_ge(v_x1, i + 1)
                pe.wait_ge(v_gc, past((i - 1) * NGATE + 1))
                for k in range(TB):
                    last = pe.transpose(xg[:, k * P:(k + 1) * P], x1st[:, k, :], ident)
                last.then_inc(e_x1, 1)

            def gate_logits(i):
                for k in range(TB):
                    for n, (l, r) in enumerate(((x1h, gh), (x1l, gh), (x1h, gl))):
                        last = pe.matmul(xg[:, k * EA:(k + 1) * EA], l[:, k * P:(k + 1) * P], r[:, :], start=n == 0, stop=n == 2)
                last.then_inc(e_gate, 1)

            def hidden(i, e):
                if e == 0:
                    pe.wait_ge(v_x1l, i + 1)
                for n in range(HC + 1):
                    q = (i * EA + e) * (HC + 1) + n
                    pe.wait_ge(v_hf, past(q - 2))
                    cols = (n * P, (HC + n) * P) if n < HC else (2 * HC * P,)
                    for which, c in enumerate(cols):
                        ws = slice(e * WC + c, e * WC + c + P)
                        o = hbank(n, which)
                        for m, (l, r) in enumerate(((wallh, x1h), (wallh, x1l), (walll, x1h))):
                            last = pe.matmul(o, l[:, ws], r[:, :], start=m == 0, stop=m == 2)
                    last.then_inc(e_h, 1)

            def down(i, e):
                q = i * EA + e
                pe.wait_ge(v_hl, (q + 1) * (HC + 1))
                pe.wait_ge(a_hh, (q + 1) * (HC + 1))
                pe.wait_ge(v_y, past(q))
                for k in range(TB):
                    cols = slice(k * P, (k + 1) * P)
                    for n in range(HC + 1):
                        rows = slice(0, P if n < HC else HT)
                        c = EA * WC + e * W2C + n * D
                        for m, (l, r) in enumerate(((hh, wallh), (hh, walll), (hl, wallh))):
                            last = pe.matmul(y[:, cols], l[rows, e % 2, n, cols], r[rows, c:c + D],
                                             start=n == 0 and m == 0, stop=n == HC and m == 2)
                last.then_inc(e_y, 1)

            def tile(i):
                hidden(i, 0)
                if not isinstance(i, int) or i > 0:
                    down(i - 1, EA - 1)
                gate_logits(i)
                for e in range(1, EA):
                    hidden(i, e)
                    if e == EA - 1 and (not isinstance(i, int) or i < NT - 1):
                        transpose_x1(i + 1)
                    down(i, e - 1)

            transpose_x1(0)
            tile(0)
            with pe.Fori(1, NT - 1) as i:
                tile(i)
            tile(NT - 1)
            down(NT - 1, EA - 1)

        @block.scalar
        def _(act):
            def exp_unit(b, par, a):
                t = b * UB + a
                k = UB * par + a
                act.wait_ge(e_tscores, t + 1)
                act.wait_ge(g_pl, past(t - 1))
                act.wait_ge(e_pv, past(t - 3))
                act.activation(p32[:, k % 2, :], ps_t[:, :], ACT.Exp, scale=SCALE).then_inc(a_p32, 1)
                act.activation(ph[:, k % 4, :], ps_t[:, :], ACT.Exp, scale=SCALE).then_inc(a_ph, 1)

            def body(b, par):
                for a in range(UB):
                    if has(b, -1) and a % 2 == 0:
                        n = b * HB - HB + a // 2
                        act.wait_ge(e_ot, n + 1)
                        act.wait_ge(e_op, past(n))
                        act.copy(oth[:, :], ps_m[:, 0:P]).then_inc(a_oth, 1)
                    if has(b, 0):
                        exp_unit(b, par, a)
                    if a == 0 and has(b, 1):
                        act.wait_ge(e_k, b + 2)
                        act.wait_ge(v_km, b + 1)
                        act.copy(kh[:, :], ps_k).then_inc(a_kh, 1)
                    if a == 1 and has(b, 1):
                        act.wait_ge(e_q, b + 2)
                        act.wait_ge(v_qa, b + 1)
                        act.copy(qh[:, :], ps_q).then_inc(a_qh, 1)
                    if a == 2 and has(b, 1):
                        act.wait_ge(e_v, b + 2)
                        act.wait_ge(e_pv, past(b * UB))
                        act.copy(vaug[:, 1 - par, :, :, 0:DH], ps_v.rearrange("p (a g d) -> p a g d", a=UB, g=NG)).then_inc(a_vh, 1)
                    if a == 3 and has(b, 2):
                        act.wait_ge(e_xt, b + 3)
                        act.wait_ge(e_v, b + 2)
                        act.copy(xth[:, W:], ps_x).then_inc(a_xh, 1)
                    if a == 3 and has(b, 0):
                        if isinstance(b, int) and b == 0:
                            act.wait_ge(ld_big, past(16 * N_BIG))
                        act.copy(wallh[:, bass.ds(b * WSTEP, WSTEP)], wall32[:, bass.ds(b * WSTEP, WSTEP)]).then_inc(a_w, 1)

            act.wait_ge(e_xt, 1)
            act.wait_ge(setup, 1)
            act.copy(xth[:, W:], ps_x).then_inc(a_xh, 1)
            pairs(act, body, 0, 0)
            act.wait_ge(v_stats, 1)
            act.sqrt(rs[:, 4, :], rs[:, 3, :]).then_inc(a_sq, 1)

            def tile(i):
                def groups(e):
                    for n in range(HC + 1):
                        q = (i * EA + e) * (HC + 1) + n
                        rows = slice(0, P if n < HC else HT)
                        act.wait_ge(e_h, q + 1)
                        act.wait_ge(v_hf, past(q - 2))
                        act.activation(sg[rows, n % 3, :], bank[n % 3][rows, 0:512], ACT.Silu).then_inc(a_silu, 1)
                        if n > 0:
                            hi(e, n - 1, q - 1)
                    hi(e, HC, q)

                def hi(e, n, q):
                    rows = slice(0, P if n < HC else HT)
                    act.wait_ge(v_hf, q + 1)
                    act.wait_ge(e_y, past(i * EA + e - 1))
                    act.copy(hh[rows, e % 2, n, :], hf[rows, n % 3, :]).then_inc(a_hh, 1)

                for e in range(EA):
                    groups(e)
                    if e == 0:
                        if not isinstance(i, int) or i > 0:
                            act.wait_ge(v_fv, past(i))
                            act.sqrt(fs[:, 4, :], fs[:, 3, :]).then_inc(a_fsq, 1)
                        act.wait_ge(v_gc, i * NGATE + 3)
                        act.activation(ex[:, :, :], ge[:, :, :], ACT.Exp).then_inc(a_ex, 1)
                    if e == EA - 1 and (not isinstance(i, int) or i < NT - 1):
                        x1_hi(i + 1)

            def x1_hi(i):
                act.wait_ge(e_x1, i + 1)
                act.wait_ge(e_h, i * EA * (HC + 1))
                act.wait_ge(e_gate, past(i))
                act.copy(x1h[:, :], bank[3][:, 512:1024]).then_inc(a_x1h, 1)

            x1_hi(0)
            tile(0)
            with act.Fori(1, NT - 1) as i:
                tile(i)
            tile(NT - 1)
            act.wait_ge(v_fv, past(NT))
            act.sqrt(fs[:, 4, :], fs[:, 3, :]).then_inc(a_fsq, 1)

        @block.vector
        def _(dve):
            links = [0]

            def link(ins):
                links[0] += 1
                ins.then_inc(v_chain, 1)
                dve.wait_ge(v_chain, links[0])

            for tile_, value in ((xth[:, 0:W], 0.0), (xtl[:, 0:W], 0.0), (kbd[:, :, :, :], 0.0), (mx[:, :, :, :, :], 0.0),
                                 (onesh[:, :], 1.0), (vaug[:, :, :, :, 2 * DH:VC], 1.0), (wqh[:, :, :, :, :], 0.0),
                                 (wql[:, :, :, :, :], 0.0), (wkh[:, :, :, :], 0.0), (wkl[:, :, :, :], 0.0), (bqr[:, :, :, :, :], 0.0),
                                 (bkr[:, :, :, :], 0.0), (bvr[:, :], 0.0), (bor[:, :], 0.0)):
                last = dve.memset(tile_, value)
            link(last)
            dve.wait_ge(ld_x, 16)
            dve.tensor_copy(xst[:, :, :], xr[:, 0:HB, :]).then_inc(v_xst, 1)
            dve.wait_ge(ld_small, 16 * N_SMALL)
            dve.tensor_copy(identb[:, :], cst[:, C_ID:C_ID + P])
            dve.tensor_scalar(nidentb[:, :], cst[:, C_ID:C_ID + P], -1.0, None, ALU.mult)
            for n, at in enumerate((C_MS, C_MS0)):
                dve.tensor_copy(mask_s[:, n, :, :], cst[:, at:at + KW].unsqueeze(1).broadcast_to([P, NG, KW]))
            for n, at in enumerate((C_MT, C_MT0)):
                dve.tensor_copy(mask_t[:, n, :, :], cst[:, at:at + W].unsqueeze(1).broadcast_to([P, 8, W]))
            dve.tensor_copy(woh[:, :, :], wo32[:, :, :])
            dve.tensor_copy(gh[:, :], g32[:, :])
            dve.tensor_copy(biash[:, :], bias32[:, :])
            link(dve.tensor_copy(wqkvh[:, :], wqkv32[:, :]))
            dve.tensor_tensor(wqkvl[:, :], wqkv32[:, :], wqkvh[:, :], ALU.subtract)
            dve.tensor_tensor(wol[:, :, :], wo32[:, :, :], woh[:, :, :], ALU.subtract)
            dve.tensor_tensor(gl[:, :], g32[:, :], gh[:, :], ALU.subtract)
            link(dve.scalar_tensor_tensor(biasm[:, :], biash[:, :], cst[0:2, C_N1:C_N1 + 1], bias32[:, :], ALU.mult, ALU.add))
            for slot in range(1, SLOTS):
                for r in range(R):
                    for dst, src in ((wqh, wqkvh), (wql, wqkvl)):
                        dve.tensor_copy(dst[:, r, :, slot, :], src[:, 0:D].rearrange("p (g r d) -> p g r d", g=NG, r=R)[:, :, r, :])
                    dve.tensor_copy(bqr[0:2, r, :, slot, :], biasm[:, 0:D].rearrange("p (g r d) -> p g r d", g=NG, r=R)[:, :, r, :])
                for dst, src in ((wkh, wqkvh), (wkl, wqkvl)):
                    dve.tensor_copy(dst[:, :, slot, :], src[:, D:D + 32].rearrange("p (g d) -> p g d", g=NG))
                dve.tensor_copy(bkr[0:2, :, slot, :], biasm[:, D:D + 32].rearrange("p (g d) -> p g d", g=NG))
            dve.memset(bkr[0:1, :, 0, 0:1], 1.0)
            dve.tensor_copy(bvr[0:2, :], biasm[:, D + 32:D + 64])
            link(dve.tensor_copy(bor[0:2, :], biasm[:, D + 64:]))
            dve.engine_nop().then_inc(setup, 1)

            def x_lo(b):
                dve.wait_ge(a_xh, b + 1)
                dve.wait_ge(e_v, past(b))
                dve.tensor_tensor(xtl[:, W:], ps_x, xth[:, W:], ALU.subtract).then_inc(v_xl, 1)

            def body(b, par):
                for a in range(UB):
                    t = b * UB + a
                    k = UB * par + a
                    nxt = (a < UB - 1 and has(b, 0)) or (a == UB - 1 and has(b, 1))
                    n = b * HB - HB + a // 2
                    if nxt:
                        dve.wait_ge(e_scores, t + 2)
                        dve.tensor_reduce(mx[:, (k + 1) % 2, :, :, 0], ps_s[:, :].rearrange("p (r g k) -> p r g k", r=2, g=NG),
                                          AX.X, ALU.max).then_inc(v_mx, 1)
                    if a % 2 == 0 and has(b, -1):
                        dve.wait_ge(a_oth, n + 1)
                        dve.tensor_tensor(otl[:, :], ps_m[:, 0:P], oth[:, :], ALU.subtract).then_inc(v_otl, 1)
                    if a % 2 == 1 and has(b, -1):
                        dve.wait_ge(e_op, n + 1)
                        dve.tensor_tensor(xr[:, bass.ds(n, 1), :], ps_m[:, 0:D].unsqueeze(1), xr[:, bass.ds(n, 1), :], ALU.add).then_inc(v_r, 1)
                    if a == 0 and has(b, 1):
                        dve.wait_ge(a_kh, b + 2)
                        dve.scalar_tensor_tensor(km[:, :], kh[:, :], cst[:, C_NK:C_NK + 1], ps_k, ALU.mult, ALU.add).then_inc(v_km, 1)
                        dve.wait_ge(v_km, b + 2)
                        dve.wait_ge(e_tscores, past(b * UB))
                        for g in range(NG):
                            rows = slice(g * 32, (g + 1) * 32)
                            last = dve.tensor_copy(kbd[rows, 1 - par, g, W:], km[rows, :])
                        last.then_inc(v_kbd, 1)
                    if a == 1 and has(b, 1):
                        dve.wait_ge(a_qh, b + 2)
                        dve.scalar_tensor_tensor(qa[:, 1 - par, :, :, :].rearrange("p a r q -> p (a r q)"), qh[:, :],
                                                 cst[:, C_NQ:C_NQ + 1], ps_q, ALU.mult, ALU.add).then_inc(v_qa, 1)
                    if a == 2 and has(b, 1):
                        dve.wait_ge(a_vh, b + 2)
                        dve.tensor_tensor(vaug[:, 1 - par, :, :, DH:2 * DH], ps_v.rearrange("p (a g d) -> p a g d", a=UB, g=NG),
                                          vaug[:, 1 - par, :, :, 0:DH], ALU.subtract).then_inc(v_vl, 1)
                        if has(b, 2):
                            dve.wait_ge(ld_x, (b + 3) * 16)
                            dve.wait_ge(e_xt, b + 2)
                            dve.tensor_scalar(xst[:, :, :], xr[:, bass.ds((b + 2) * HB, HB), :], 1.0, None, ALU.mult).then_inc(v_xst, 1)
                    if a % 2 == 1 and has(b, -1):
                        dve.wait_ge(v_r, n + 1)
                    if nxt:
                        dve.wait_ge(e_maxt, t + 2)
                        dve.wait_ge(e_tscores, past(t))
                        nb, na = (par, a + 1) if a < UB - 1 else (1 - par, 0)
                        dve.tensor_tensor(qm[:, (k + 1) % 2, :, :], ps_m.rearrange("p (r q) -> p r q", r=R),
                                          qa[:, nb, na, :, :], ALU.add).then_inc(v_qm, 1)
                    if a % 2 == 1 and has(b, -1):
                        dve.bn_stats(stats[:, bass.ds(n, 1), :].rearrange("p o c -> p (o c)"), xr[:, bass.ds(n, 1), :].rearrange("p o d -> p (o d)")).then_inc(v_chain, 1)
                    if (a == 3 and has(b, 0)) or (a == 1 and has(b, -1)):
                        m = b * HB + (0 if a == 3 else -1)
                        dve.wait_ge(e_pv, (m + 1) * 2)
                        o = ps_o.rearrange("p (n c) -> p n c", c=VC)
                        dve.reciprocal(rden[:, :], o[:, :, 2 * DH]).then_inc(v_rden, 1)
                        dve.wait_ge(v_rden, m + 1)
                        dve.wait_ge(g_o, past(m))
                        dve.tensor_tensor(ot2[:, :, :], o[:, :, 0:2 * DH], rden[:, :].unsqueeze(2).broadcast_to([P, 16, 2 * DH]), ALU.mult).then_inc(v_o, 1)
                    if a == 3 and has(b, 2):
                        x_lo(b + 2)
                    if a == 3 and has(b, 0):
                        dve.wait_ge(a_w, b + 1)
                        dve.tensor_tensor(walll[:, bass.ds(b * WSTEP, WSTEP)], wall32[:, bass.ds(b * WSTEP, WSTEP)],
                                          wallh[:, bass.ds(b * WSTEP, WSTEP)], ALU.subtract).then_inc(v_w, 1)

            x_lo(0)
            dve.wait_ge(ld_x, 32)
            dve.wait_ge(e_xt, 1)
            pairs(dve, body, 0, 0)

            links[0] += NBLK
            dve.wait_ge(v_chain, links[0])

            def moments(st, t, mean):
                half = 0.5
                link(dve.tensor_tensor(t[:, 1, :], st[:, :, 1], st[:, :, 4], ALU.subtract))
                dve.tensor_tensor(t[:, 0, :], st[:, :, 1], st[:, :, 4], ALU.add)
                link(dve.tensor_tensor(t[:, 2, :], t[:, 1, :], t[:, 1, :], ALU.mult))
                link(dve.tensor_tensor(t[:, 3, :], st[:, :, 2], st[:, :, 5], ALU.add))

            t = rs
            link(dve.tensor_tensor(t[:, 1, :], stats[:, :, 1], stats[:, :, 4], ALU.subtract))
            link(dve.tensor_tensor(t[:, 0, :], stats[:, :, 1], stats[:, :, 4], ALU.add))
            link(dve.tensor_tensor(t[:, 2, :], t[:, 1, :], t[:, 1, :], ALU.mult))
            link(dve.tensor_tensor(t[:, 3, :], stats[:, :, 2], stats[:, :, 5], ALU.add))
            link(dve.scalar_tensor_tensor(t[:, 1, :], t[:, 2, :], D / 4.0, t[:, 3, :], ALU.mult, ALU.add))
            link(dve.tensor_scalar(t[:, 3, :], t[:, 1, :], 1.0 / D, EPS, ALU.mult, ALU.add))
            dve.engine_nop().then_inc(v_stats, 1)
            dve.wait_ge(a_sq, 1)
            link(dve.reciprocal(t[:, 5, :], t[:, 4, :]))
            link(dve.tensor_tensor(t[:, 1, :], t[:, 5, :], t[:, 5, :], ALU.mult))
            link(dve.tensor_tensor(t[:, 2, :], t[:, 1, :], t[:, 3, :], ALU.mult))
            link(dve.tensor_scalar(t[:, 1, :], t[:, 2, :], -0.5, 1.5, ALU.mult, ALU.add))
            link(dve.tensor_tensor(rstd[:, :], t[:, 5, :], t[:, 1, :], ALU.mult))
            link(dve.scalar_tensor_tensor(nmr[:, :], t[:, 0, :], -0.5, rstd[:, :], ALU.mult, ALU.mult))
            base = links[0]

            CH = TB + 1 + 8 + 3 + TB + 5 + 5

            def x1_norm(i, count):
                for k in range(TB):
                    blk = i * TB + k
                    last = dve.tensor_scalar(xr[:, bass.ds(blk, 1), :].rearrange("p o d -> p (o d)"), xr[:, bass.ds(blk, 1), :].rearrange("p o d -> p (o d)"),
                                             rstd[:, bass.ds(blk, 1)], nmr[:, bass.ds(blk, 1)], ALU.mult, ALU.add)
                    last.then_inc(v_x1n, 1)
                dve.wait_ge(v_x1n, (i + 1) * TB)
                dve.wait_ge(e_x1, past(i))
                dve.tensor_scalar(x1st[:, :, :], xr[:, bass.ds(i * TB, TB), :], 1.0, None, ALU.mult).then_inc(v_x1, 1)

            def x1_lo(i):
                dve.wait_ge(a_x1h, i + 1)
                dve.tensor_tensor(x1l[:, :], bank[3][:, 512:1024], x1h[:, :], ALU.subtract).then_inc(v_x1l, 1)

            def groups(i, e):
                def lo(n, q):
                    rows = slice(0, P if n < HC else HT)
                    dve.wait_ge(a_hh, q + 1)
                    dve.tensor_tensor(hl[rows, e % 2, n, :], hf[rows, n % 3, :], hh[rows, e % 2, n, :], ALU.subtract).then_inc(v_hl, 1)
                for n in range(HC + 1):
                    q = (i * EA + e) * (HC + 1) + n
                    rows = slice(0, P if n < HC else HT)
                    w3part = bank[n % 3][:, 512:1024] if n < HC else bank[n % 3][HT:P, 0:512]
                    dve.wait_ge(a_silu, q + 1)
                    dve.wait_ge(v_hl, past(q - 2))
                    dve.wait_ge(a_hh, past(q - 2))
                    dve.tensor_tensor(hf[rows, n % 3, :], w3part, sg[rows, n % 3, :], ALU.mult).then_inc(v_hf, 1)
                    if n > 0:
                        lo(n - 1, q - 1)
                lo(HC, q)

            def combine(i, e):
                dve.wait_ge(e_y, i * EA + e + 1)
                for k in range(TB):
                    blk = i * TB + k
                    to = yst[:, k, :] if e == EA - 1 else xr[:, bass.ds(blk, 1), :].rearrange("p o d -> p (o d)")
                    last = dve.scalar_tensor_tensor(to, bank[3][:, k * D:(k + 1) * D], cw[:, k, e:e + 1],
                                                    xr[:, bass.ds(blk, 1), :].rearrange("p o d -> p (o d)"), ALU.mult, ALU.add)
                last.then_inc(v_y, 1)

            class Chain:
                def __init__(self, s, i, ch, first):
                    self.s, self.i, self.ch, self.n, self.first = s, i, ch, 0, first

                def __call__(self, ins):
                    self.n += 1
                    ins.then_inc(self.s, 1)
                    dve.wait_ge(self.s, self.i * self.ch + self.n)

            

            def gate_weights(i):
                c = Chain(v_gc, i, NGATE, 0)
                dve.wait_ge(e_gate, i + 1)
                c(dve.tensor_copy(lg[:, :, :], bank[3][:, 512:512 + TB * EA].rearrange("p (k e) -> p k e", k=TB)))
                li = lg[:, :, :].unsqueeze(3).broadcast_to([P, TB, EA, EA])
                lj = lg[:, :, :].unsqueeze(2).broadcast_to([P, TB, EA, EA])
                tri = cst[:, C_TRI:C_TRI + EA * EA].rearrange("p (a b) -> p a b", a=EA).unsqueeze(1).broadcast_to([P, TB, EA, EA])
                c(dve.tensor_reduce(gm[:, :], lg[:, :, :], AX.X, ALU.max))
                c(dve.tensor_tensor(ge[:, :, :], lg[:, :, :], gm[:, :].unsqueeze(2).broadcast_to([P, TB, EA]), ALU.subtract))
                c(dve.tensor_tensor(gt[:, :, :, :], lj, li, ALU.is_gt))
                c(dve.tensor_tensor(eq[:, :, :, :], lj, li, ALU.is_equal))
                c(dve.tensor_tensor(eq[:, :, :, :], eq[:, :, :, :], tri, ALU.mult))
                c(dve.tensor_tensor(gt[:, :, :, :], gt[:, :, :, :], eq[:, :, :, :], ALU.add))
                c(dve.tensor_reduce(rank[:, :, :], gt[:, :, :, :], AX.X, ALU.add))
                dve.wait_ge(a_ex, i + 1)
                c(dve.scalar_tensor_tensor(cwu[:, :, :], rank[:, :, :], TOPK - 0.5, ex[:, :, :], ALU.is_lt, ALU.mult))
                c(dve.tensor_reduce(gs[:, :], cwu[:, :, :], AX.X, ALU.add))
                c(dve.reciprocal(gr[:, :], gs[:, :]))
                c(dve.tensor_tensor(cw[:, :, :], cwu[:, :, :], gr[:, :].unsqueeze(2).broadcast_to([P, TB, EA]), ALU.mult))
                assert c.n == NGATE

            def final(i):
                c = Chain(v_fc, i, NFIN, 0)
                dve.wait_ge(v_y, (i + 1) * EA)
                for k in range(TB):
                    last = dve.bn_stats(fst[:, k, :], yst[:, k, :])
                c(last)
                c(dve.tensor_tensor(fs[:, 1, :], fst[:, :, 1], fst[:, :, 4], ALU.subtract))
                c(dve.tensor_tensor(fs[:, 0, :], fst[:, :, 1], fst[:, :, 4], ALU.add))
                c(dve.tensor_tensor(fs[:, 2, :], fs[:, 1, :], fs[:, 1, :], ALU.mult))
                c(dve.tensor_tensor(fs[:, 5, :], fst[:, :, 2], fst[:, :, 5], ALU.add))
                c(dve.scalar_tensor_tensor(fs[:, 1, :], fs[:, 2, :], D / 4.0, fs[:, 5, :], ALU.mult, ALU.add))
                dve.tensor_scalar(fs[:, 3, :], fs[:, 1, :], 1.0 / D, EPS, ALU.mult, ALU.add).then_inc(v_fv, 1)
                dve.wait_ge(a_fsq, i + 1)
                c(dve.reciprocal(fs[:, 5, :], fs[:, 4, :]))
                c(dve.tensor_tensor(fs[:, 1, :], fs[:, 5, :], fs[:, 5, :], ALU.mult))
                c(dve.tensor_tensor(fs[:, 2, :], fs[:, 1, :], fs[:, 3, :], ALU.mult))
                c(dve.tensor_scalar(fs[:, 1, :], fs[:, 2, :], -0.5, 1.5, ALU.mult, ALU.add))
                c(dve.tensor_tensor(frs[:, :], fs[:, 5, :], fs[:, 1, :], ALU.mult))
                c(dve.scalar_tensor_tensor(fnm[:, :], fs[:, 0, :], -0.5, frs[:, :], ALU.mult, ALU.mult))
                assert c.n == NFIN
                dve.wait_ge(st_out, past(i * 16))
                for k in range(TB):
                    last = dve.tensor_scalar(ost[:, k, :], yst[:, k, :], frs[:, k:k + 1], fnm[:, k:k + 1], ALU.mult, ALU.add)
                last.then_inc(v_out, 1)

            def tile(i):
                inner = not isinstance(i, int)
                groups(i, 0)
                if inner or i > 0:
                    combine(i - 1, EA - 1)
                    final(i - 1)
                gate_weights(i)
                for e in range(1, EA):
                    groups(i, e)
                    if e == 2 and (inner or i < NT - 1):
                        x1_norm(i + 1, 0)
                    if e == EA - 1 and (inner or i < NT - 1):
                        x1_lo(i + 1)
                    combine(i, e - 1)

            x1_norm(0, 0)
            x1_lo(0)
            tile(0)
            with dve.Fori(1, NT - 1) as i:
                tile(i)
            tile(NT - 1)
            combine(NT - 1, EA - 1)
            final(NT - 1)


def constants():
    import numpy as np
    c = np.zeros((P, C_ALL), np.float32)
    c[:, C_ID:C_ID + P] = np.eye(P)
    q = np.arange(P)[:, None] % W
    key = np.arange(KW)[None, :]
    seen = (key > q) & (key <= W + q)
    c[:, C_MS:C_MS + KW] = np.where(seen, 0, -1e30)
    c[:, C_MS0:C_MS0 + KW] = np.where(seen & (key >= W), 0, -1e30)
    c[:, C_MT:C_MT + W] = c[0:W, C_MS:C_MS + KW].T
    c[:, C_MT0:C_MT0 + W] = c[0:W, C_MS0:C_MS0 + KW].T
    slot = np.arange(P) % 32 // DH
    c[:, C_NQ] = -1.0 * (slot == 2)
    c[:, C_NK] = -1.0 * (slot == 3)
    c[1, C_N1] = -1.0
    i, j = np.arange(EA)[:, None], np.arange(EA)[None, :]
    c[:, C_TRI:] = (j < i).astype(np.float32).reshape(-1)
    return c


def kernel(L0_attn_x, L0_attn_Wq, L0_attn_bq, L0_attn_Wk, L0_attn_bk, L0_attn_Wv, L0_attn_bv, L0_attn_Wo, L0_attn_bo,
           L0_ffn_gate_w, L0_ffn_w1, L0_ffn_w2, L0_ffn_w3):
    import numpy as np
    import concourse.bacc as bacc
    from concourse.bass_utils import run_bass_kernel_spmd

    nc = bacc.Bacc("TRN2", target_bir_lowering=False, num_devices=1)
    named = {"x": L0_attn_x, "wq": L0_attn_Wq, "bq": L0_attn_bq, "wk": L0_attn_Wk, "bk": L0_attn_bk, "wv": L0_attn_Wv,
             "bv": L0_attn_bv, "wo": L0_attn_Wo, "bo": L0_attn_bo, "gate": L0_ffn_gate_w, "w1": L0_ffn_w1, "w2": L0_ffn_w2,
             "w3": L0_ffn_w3, "const": constants()}
    arrays, args = {}, []
    for name, a in named.items():
        a = np.ascontiguousarray(a)
        arrays[f"in_{name}"] = a
        args.append(nc.dram_tensor(f"in_{name}", a.shape, mybir.dt.from_np(a.dtype), kind="ExternalInput").ap())
    o = nc.dram_tensor("out", (NBLK, P, D), F32, kind="ExternalOutput").ap()
    build(nc, *args, o)
    r = run_bass_kernel_spmd(nc, [arrays], core_ids=[0])
    return r.results[0]["out"].reshape(B, S, D)
```

```python
from contextlib import ExitStack

import concourse.bass as bass
from concourse import mybir

F32 = mybir.dt.float32
F16 = mybir.dt.float16
BF16 = mybir.dt.bfloat16
ALU = mybir.AluOpType
ACT = mybir.ActivationFunctionType
AX = mybir.AxisListType

P = 128
B, S, D = 32, 256, 128
NH, NG, DH = 16, 4, 8
R = NH // NG
W = 64
UB = S // W
KW = 2 * W
HB = S // P
NBLK = B * HB
SLOTS = 4
VC = 2 * DH + 1
E, EA, TOPK = 8, 4, 2
H = 704
HC = H // P
HT = H - HC * P
WC = 2 * H
W2C = (HC + 1) * D
WALL = EA * (WC + W2C)
WSTEP = WALL // B
TB = 4
TT = TB * P
NGATE, NFIN = 12, 12
NT = NBLK // TB
SCALE = float(DH) ** -0.5
EPS = 1e-5
C_ID, C_MS, C_MS0, C_MT, C_MT0, C_NQ, C_NK, C_N1, C_TRI = 0, 128, 256, 384, 448, 512, 513, 514, 515
C_ALL = C_TRI + EA * EA
assert WALL % B == 0 and HT * 2 == P


def build(nc, x, wq, bq, wk, bk, wv, bv, wo, bo, gate, w1, w2, w3, const, out):
    ctx = ExitStack()
    with ctx:
        def sb(name, shape, dt):
            return ctx.enter_context(nc.sbuf_tensor(name, shape, dt))

        def pb(name, shape, dt=F32):
            return ctx.enter_context(nc.psum_tensor(name, shape, dt))

        def sem(name):
            return ctx.enter_context(nc.semaphore(name))

        xr = sb("xr", [P, NBLK, D], F32)
        stats = sb("stats", [P, NBLK, 6], F32)
        wall32 = sb("wall32", [P, WALL], F32)
        wallh = sb("wallh", [P, WALL], F16)
        walll = sb("walll", [P, WALL], F16)
        cst = sb("cst", [P, C_ALL], F32)
        identb = sb("identb", [P, P], BF16)
        nidentb = sb("nidentb", [P, P], BF16)
        onesh = sb("onesh", [P, S], F16)
        mask_s = sb("mask_s", [P, 2, NG, KW], BF16)
        mask_t = sb("mask_t", [P, 2, 8, W], BF16)
        wqkv32 = sb("wqkv32", [P, D + 2 * NG * DH], F32)
        wqkvh = sb("wqkvh", [P, D + 2 * NG * DH], F16)
        wqkvl = sb("wqkvl", [P, D + 2 * NG * DH], F16)
        wqh = sb("wqh", [P, R, NG, SLOTS, DH], F16)
        wql = sb("wql", [P, R, NG, SLOTS, DH], F16)
        wkh = sb("wkh", [P, NG, SLOTS, DH], F16)
        wkl = sb("wkl", [P, NG, SLOTS, DH], F16)
        wo32 = sb("wo32", [P, 2, D], F32)
        woh = sb("woh", [P, 2, D], F16)
        wol = sb("wol", [P, 2, D], F16)
        bias32 = sb("bias32", [2, 2 * D + 2 * NG * DH], F32)
        biash = sb("biash", [2, 2 * D + 2 * NG * DH], F16)
        biasm = sb("biasm", [2, 2 * D + 2 * NG * DH], F16)
        bqr = sb("bqr", [P, R, NG, SLOTS, DH], F16)
        bkr = sb("bkr", [P, NG, SLOTS, DH], F16)
        bvr = sb("bvr", [P, NG * DH], F16)
        bor = sb("bor", [P, D], F16)
        g32 = sb("g32", [P, EA], F32)
        gh = sb("gh", [P, EA], F16)
        gl = sb("gl", [P, EA], F16)
        xst = sb("xst", [P, HB, D], F32)
        xth = sb("xth", [P, W + S], F16)
        xtl = sb("xtl", [P, W + S], F16)
        qh = sb("qh", [P, R * S], F16)
        qa = sb("qa", [P, 2, UB, R, W], F16)
        kh = sb("kh", [P, S], F16)
        km = sb("km", [P, S], F16)
        kbd = sb("kbd", [P, 2, NG, W + S], F16)
        vaug = sb("vaug", [P, 2, UB, NG, VC], F16)
        mx = sb("mx", [P, 2, 2, NG, 32], BF16)
        qm = sb("qm", [P, 2, R, W], F16)
        p32 = sb("p32", [P, 2, NH * W], F32)
        ph = sb("ph", [P, 4, NH * W], F16)
        pl = sb("pl", [P, 4, NH * W], F16)
        rden = sb("rden", [P, 2 * 8], F32)
        ot2 = sb("ot2", [P, 2 * 8, 2 * DH], F32)
        o32 = sb("o32", [P, 2 * 8, DH], F32)
        oth = sb("oth", [P, P], F16)
        otl = sb("otl", [P, P], F16)
        rs = sb("rs", [P, 6, NBLK], F32)
        rstd = sb("rstd", [P, NBLK], F32)
        nmr = sb("nmr", [P, NBLK], F32)
        x1st = sb("x1st", [P, TB, D], F32)
        x1h = sb("x1h", [P, TT], F16)
        x1l = sb("x1l", [P, TT], F16)
        sg = sb("sg", [P, 3, TT], F32)
        hf = sb("hf", [P, 3, TT], F32)
        nh = (HC + 1) * TT
        hh, hl = (wall32[:, n * nh:(n + 1) * nh].bitcast(F16).rearrange("p (b c t) -> p b c t", b=2, c=HC + 1) for n in range(2))
        lg = sb("lg", [P, TB, EA], F32)
        gt = sb("gt", [P, TB, EA, EA], F32)
        eq = sb("eq", [P, TB, EA, EA], F32)
        rank = sb("rank", [P, TB, EA], F32)
        gm = sb("gm", [P, TB], F32)
        ge = sb("ge", [P, TB, EA], F32)
        ex = sb("ex", [P, TB, EA], F32)
        cwu = sb("cwu", [P, TB, EA], F32)
        gs = sb("gs", [P, TB], F32)
        gr = sb("gr", [P, TB], F32)
        cw = sb("cw", [P, TB, EA], F32)
        fst = sb("fst", [P, TB, 6], F32)
        fs = sb("fs", [P, 6, TB], F32)
        frs = sb("frs", [P, TB], F32)
        fnm = sb("fnm", [P, TB], F32)
        yst = sb("yst", [P, TB, D], F32)
        ost = sb("ost", [P, TB, D], F32)
        bank = [pb(f"bank{i}", [P, 1024]) for i in range(4)]
        ps_s, ps_t = bank[0], bank[1]
        b45, b67 = bank[2], bank[3]
        ps_m = b45[:, 0:R * W]
        ps_o = b45[:, 512:512 + 2 * 8 * VC]
        ps_x, ps_k, ps_v, ps_q = b67[:, 0:S], b67[:, 0:S], b67[:, 512:512 + UB * NG * DH], b67[:, :]

        ld_x = sem("ld_x")
        ld_xst = sem("ld_xst")
        ld_cst = sem("ld_cst")
        ld_small = sem("ld_small")
        v_zero = sem("v_zero")
        v_pad = sem("v_pad")
        ld_big = sem("ld_big")
        st_out = sem("st_out")
        setup = sem("setup")
        e_scores, e_maxt, e_tscores, e_pv = sem("e_scores"), sem("e_maxt"), sem("e_tscores"), sem("e_pv")
        e_xt, e_k, e_q, e_v, e_ot, e_op = (sem(n) for n in ("e_xt", "e_k", "e_q", "e_v", "e_ot", "e_op"))
        a_xh, a_kh, a_qh, a_vh, a_oth, a_p32, a_ph, a_w = (
            sem(n) for n in ("a_xh", "a_kh", "a_qh", "a_vh", "a_oth", "a_p32", "a_ph", "a_w"))
        v_xl, v_km, v_kbd, v_qa, v_vl, v_mx, v_qm, v_rden, v_o, v_otl, v_r, v_w = (
            sem(n) for n in ("v_xl", "v_km", "v_kbd", "v_qa", "v_vl", "v_mx", "v_qm", "v_rden",
                             "v_o", "v_otl", "v_r", "v_w"))
        g_pl, g_o = sem("g_pl"), sem("g_o")
        v_chain = sem("v_chain")
        v_stats, v_x1n, v_gc, v_fc = (sem(n) for n in ("v_stats", "v_x1n", "v_gc", "v_fc"))
        a_sq = sem("a_sq")
        e_x1, e_gate, e_h, e_y = sem("e_x1"), sem("e_gate"), sem("e_h"), sem("e_y")
        a_x1h, a_silu, a_hh, a_ex, a_fsq = (sem(n) for n in ("a_x1h", "a_silu", "a_hh", "a_ex", "a_fsq"))
        v_x1, v_x1l, v_hf, v_hl, v_y, v_fv, v_out = (
            sem(n) for n in ("v_x1", "v_x1l", "v_hf", "v_hl", "v_y", "v_fv", "v_out"))

        def past(n):
            return max(n, 0) if isinstance(n, int) else n

        block = ctx.enter_context(nc.Block())

        def pairs(eng, body, lo, hi):
            for b in (-1, 0, 1):
                body(b, b % 2)
            with eng.Fori(1, B // 2 - 1) as i:
                for par in range(2):
                    body(i * 2 + par, par)
            for b in (B - 2, B - 1, B, B + 1):
                body(b, b % 2)

        def has(b, k):
            return not isinstance(b, int) or 0 <= b + k < B

        @block.sync
        def _(sp):
            sp.dma_start(xr[:, 0:HB, :], x[0].rearrange("(h p) d -> p h d", p=P)).then_inc(ld_x, 16)
            sp.dma_start(xst[:, :, :], x[0].rearrange("(h p) d -> p h d", p=P)).then_inc(ld_xst, 16)
            sp.dma_start(cst[:, :], const).then_inc(ld_cst, 16)
            sp.dma_start(wqkv32[:, 0:D], wq).then_inc(ld_small, 16)
            sp.dma_start(wqkv32[:, D:D + 32], wk).then_inc(ld_small, 16)
            sp.dma_start(wqkv32[:, D + 32:D + 64], wv).then_inc(ld_small, 16)
            for at, n, bias in ((0, D, bq), (D, 32, bk), (D + 32, 32, bv), (D + 64, D, bo)):
                sp.dma_start(bias32[:, at:at + n], bias.unsqueeze(0).broadcast_to([2, n])).then_inc(ld_small, 16)
            for half in range(2):
                for r1 in range(2):
                    sp.dma_start(wo32[half * 64:(half + 1) * 64, r1, :],
                                 wo.rearrange("(m r d) n -> r m d n", r=2, d=DH)[r1]).then_inc(ld_small, 16)
            sp.dma_start(g32[:, :], gate[0:EA, :].rearrange("e d -> d e"), allow_slow_non_contiguous=True).then_inc(ld_small, 16)
            sp.dma_start(xr[:, HB:2 * HB, :], x[1].rearrange("(h p) d -> p h d", p=P)).then_inc(ld_x, 16)
            sp.wait_ge(v_zero, 1)
            for e in range(EA):
                c = e * WC
                sp.dma_start(wall32[:, c:c + HC * P], w1[e, :, 0:HC * P]).then_inc(ld_big, 16)
                sp.dma_start(wall32[:, c + HC * P:c + 2 * HC * P], w3[e, :, 0:HC * P]).then_inc(ld_big, 16)
                sp.dma_start(wall32[:, c + 2 * HC * P:c + 2 * HC * P + HT], w1[e, :, HC * P:H]).then_inc(ld_big, 16)
                sp.dma_start(wall32[:, c + 2 * HC * P + HT:c + WC], w3[e, :, HC * P:H]).then_inc(ld_big, 16)
                c = EA * WC + e * W2C
                sp.dma_start(wall32[:, c:c + HC * D].rearrange("p (k d) -> p k d", k=HC),
                             w2[e, 0:HC * P, :].rearrange("(k p) d -> p k d", p=P)).then_inc(ld_big, 16)
                sp.dma_start(wall32[0:HT, c + HC * D:c + W2C], w2[e, HC * P:H, :]).then_inc(ld_big, 16)
            with sp.Fori(2, B) as b:
                sp.wait_ge(ld_x, b * 16)
                sp.dma_start(xr[:, bass.ds(b * HB, HB), :],
                             x[bass.ds(b, 1)].rearrange("o (h p) d -> p (o h) d", p=P)).then_inc(ld_x, 16)
            with sp.Fori(1, NT + 1) as i:
                sp.wait_ge(v_out, i)
                sp.dma_start(out[bass.ds(i * TB - TB, TB)].rearrange("k p d -> p k d"), ost[:, :, :]).then_inc(st_out, 16)
            sp.wait_ge(st_out, 16 * NT)

        N_SMALL = 3 + 4 + 4 + 1
        N_BIG = EA * 6

        @block.gpsimd
        def _(pool):
            tails = wall32[HT:P, EA * WC:].rearrange("p (e c) -> p e c", e=EA)[:, :, HC * D:]
            pool.memset(tails, 0.0).then_inc(v_zero, 1)

            def body(b, par):
                def lo_part(t, k):
                    pool.wait_ge(a_ph, t + 1)
                    pool.wait_ge(e_pv, past(t - 3))
                    pool.tensor_tensor(pl[:, k % 4, :], p32[:, k % 2, :], ph[:, k % 4, :], ALU.subtract).then_inc(g_pl, 1)

                def sum_o(n):
                    pool.wait_ge(v_o, n + 1)
                    pool.wait_ge(e_ot, past(n))
                    pool.tensor_tensor(o32[:, :, :], ot2[:, :, 0:DH], ot2[:, :, DH:2 * DH], ALU.add).then_inc(g_o, 1)

                for s in range(UB):
                    if s in (0, 2) and has(b, -1):
                        sum_o(b * HB - HB + s // 2)
                    if s == 0 and has(b, -1):
                        pool.wait_ge(a_w, b)
                    if has(b, 0):
                        lo_part(b * UB + s, UB * par + s)
                    if s == 0 and has(b, -1):
                        share = bass.ds(b * WSTEP - WSTEP, WSTEP)
                        pool.tensor_tensor(walll[:, share], wall32[:, share], wallh[:, share], ALU.subtract).then_inc(v_w, 1)
            pairs(pool, body, 0, 0)

        @block.tensor
        def _(pe):
            def transpose_x(b):
                pe.wait_ge(ld_xst, 16 * b + 16)
                pe.wait_ge(v_qa, past(2 * b - 1))
                for h in range(HB):
                    last = pe.transpose(ps_x[:, h * P:(h + 1) * P], xst[:, h, :], cst[:, C_ID:C_ID + P])
                last.then_inc(e_xt, 1)

            def project_k(b):
                pe.wait_ge(setup, 1)
                pe.wait_ge(v_xl, b + 1)
                pe.wait_ge(a_xh, b + 1)
                pe.wait_ge(v_qa, past(2 * b))
                for n, (w, m) in enumerate(((bkr, onesh[:, 0:S]), (wkh, xth[:, W:]), (wkh, xtl[:, W:]), (wkl, xth[:, W:]))):
                    last = pe.matmul(ps_k, w[:, :, :, :].rearrange("p g s d -> p (g s d)"), m, start=n == 0, stop=n == 3)
                last.then_inc(e_k, 1)

            def project_q(b):
                pe.wait_ge(v_km, b + 1)
                pe.wait_ge(v_vl, b + 1)
                for j in range(2):
                    cols = slice(W + j * P, W + (j + 1) * P)
                    for r in range(R):
                        o = ps_q[:, j * 512:(j + 1) * 512].rearrange("p (a r q) -> p a r q", a=2, r=R)[:, :, r, :]
                        for n, (w, m) in enumerate(((bqr, onesh[:, 0:P]), (wqh, xth[:, cols]), (wqh, xtl[:, cols]), (wql, xth[:, cols]))):
                            last = pe.matmul(o, w[:, r, :, :, :].rearrange("p g s d -> p (g s d)"), m, start=n == 0, stop=n == 3)
                last.then_inc(e_q, 1)

            def project_v(b):
                for a in range(UB):
                    o = ps_v[:, a * 32:(a + 1) * 32]
                    win = slice(a * W, a * W + KW)
                    for n, (l, r) in enumerate(((onesh[:, 0:P], bvr[:, :]), (xth[:, win], wqkvh[:, D + 32:]),
                                                (xtl[:, win], wqkvh[:, D + 32:]), (xth[:, win], wqkvl[:, D + 32:]))):
                        last = pe.matmul(o, l, r, start=n == 0, stop=n == 3)
                last.then_inc(e_v, 1)

            def scores(b, par, a):
                t = b * UB + a
                if a % 2 == 0:
                    pe.wait_ge(v_qa, b * 2 + a // 2 + 1)
                if a == 0:
                    pe.wait_ge(v_kbd, b + 1)
                pe.wait_ge(v_mx, past(t))
                for rp in range(2):
                    o = ps_s[:, rp * 512:(rp + 1) * 512]
                    pe.matmul(o, identb[:, :], mask_s[:, int(a == 0), :, :].rearrange("p g k -> p (g k)"), start=True, stop=False)
                    last = pe.matmul(o, qa[:, par, a, 2 * rp:2 * rp + 2, :].rearrange("p r q -> p (r q)"),
                                     kbd[:, par, :, a * W:a * W + KW], start=False, stop=True)
                last.then_inc(e_scores, 1)

            def max_rows(t, k):
                pe.wait_ge(v_mx, t + 1)
                pe.wait_ge(v_qm, past(t))
                for rp in range(2):
                    last = pe.matmul(ps_m[:, rp * P:(rp + 1) * P], mx[:, k % 2, rp, :, :].rearrange("p g c -> p (g c)"),
                                     nidentb[:, :], start=True, stop=True)
                last.then_inc(e_maxt, 1)

            def tscores(b, par, a):
                t = b * UB + a
                pe.wait_ge(v_qm, t + 1)
                pe.wait_ge(a_ph, past(t))
                for j in range(2):
                    o = ps_t[:, j * 512:(j + 1) * 512]
                    pe.matmul(o, identb[:, :], mask_t[:, int(a == 0), :, :].rearrange("p h q -> p (h q)"), start=True, stop=False)
                    for g in (2 * j, 2 * j + 1):
                        last = pe.matmul(ps_t[:, g * 256:(g + 1) * 256], kbd[:, par, g, a * W:a * W + KW],
                                         qm[:, a % 2, :, :].rearrange("p r q -> p (r q)"), start=False, stop=g % 2 == 1)
                last.then_inc(e_tscores, 1)

            def pv(b, par, a):
                t = b * UB + a
                pe.wait_ge(g_pl, t + 1)
                pe.wait_ge(a_ph, t + 1)
                pe.wait_ge(v_vl, b + 1)
                pe.wait_ge(v_o, past(b * HB + a // 2))
                k = (UB * par + a) % 4
                for g in range(NG):
                    for rp in range(2):
                        n = (a % 2) * 8 + g * 2 + rp
                        c = (g * 2 + rp) * P
                        pe.matmul(ps_o[:, n * VC:(n + 1) * VC], ph[:, k, c:c + P], vaug[:, par, a, g, :], start=True, stop=False)
                        last = pe.matmul(ps_o[:, n * VC:(n + 1) * VC], pl[:, k, c:c + P], vaug[:, par, a, g, :], start=False, stop=True)
                last.then_inc(e_pv, 1)

            def transpose_o(n):
                pe.wait_ge(g_o, n + 1)
                pe.wait_ge(v_r, past(n))
                pe.transpose(ps_m[:, 0:P], o32[:, :, :].rearrange("p a b -> p (a b)"), cst[:, C_ID:C_ID + P]).then_inc(e_ot, 1)

            def project_o(n):
                pe.wait_ge(v_otl, n + 1)
                pe.matmul(ps_m[:, 0:D], onesh[:, 0:P], bor[:, :], start=True, stop=True)
                for m, (l, r) in enumerate(((oth, woh), (otl, woh), (oth, wol))):
                    for r1 in range(2):
                        for u in range(2):
                            rows = slice(u * 64, (u + 1) * 64)
                            last = pe.matmul(ps_m[rows, 0:D], l[rows, r1 * 64:(r1 + 1) * 64], r[rows, r1, :],
                                             start=False, stop=m == 2 and r1 == 1, skip_group_check=True)
                last.then_inc(e_op, 1)

            def body(b, par):
                for a in range(UB):
                    t = b * UB + a
                    k = par * UB + a
                    if a < UB - 1 and has(b, 0):
                        scores(b, par, a + 1)
                    if a == UB - 1 and has(b, 1):
                        scores(b + 1, 1 - par, 0)
                    if a < 2 and has(b, -1):
                        pv(b - 1, 1 - par, a + 2)
                    if a >= 2 and has(b, 0):
                        pv(b, par, a - 2)
                    if has(b, 0) and (has(b, -1) if a else has(b, -2)):
                        pe.wait_ge(v_qm, t + 1)
                    if a % 2 == 1 and has(b, -1):
                        transpose_o(b * HB - HB + a // 2)
                    if a == 2 and has(b, -1):
                        project_o(b * HB - HB)
                    if a == 0 and has(b, -2):
                        project_o(b * HB - HB - 1)
                    if a == 3 and has(b, 2):
                        transpose_x(b + 2)
                    if has(b, 0):
                        tscores(b, par, a)
                    if (a < UB - 1 and has(b, 0)) or (a == UB - 1 and has(b, 1)):
                        if a % 2 == 1 and has(b, -1):
                            pe.wait_ge(v_otl, b * HB - HB + a // 2 + 1)
                        if a == 2 and has(b, -1):
                            pe.wait_ge(v_r, b * HB - HB + 1)
                        if a == 0 and has(b, -2):
                            pe.wait_ge(v_r, b * HB - HB)
                        max_rows(t + 1, k + 1)
                    if a == 0 and has(b, 1):
                        project_k(b + 1)
                        project_v(b + 1)
                    if a == 1 and has(b, 1):
                        project_q(b + 1)

            pe.wait_ge(ld_cst, 16)
            transpose_x(0)
            pairs(pe, body, 0, 0)

            pe.wait_ge(v_w, B)
            ident = cst[:, C_ID:C_ID + P]
            b01, b23, b45_, b67_ = bank

            def hbank(n, which):
                return bank[n % 3][:, which * 512:(which + 1) * 512]

            y = bank[3][:, 0:512]
            xg = bank[3][:, 512:1024]

            def transpose_x1(i):
                pe.wait_ge(v_x1, i + 1)
                pe.wait_ge(v_gc, past((i - 1) * NGATE + 1))
                for k in range(TB):
                    last = pe.transpose(xg[:, k * P:(k + 1) * P], x1st[:, k, :], ident)
                last.then_inc(e_x1, 1)

            def gate_logits(i):
                for k in range(TB):
                    for n, (l, r) in enumerate(((x1h, gh), (x1l, gh), (x1h, gl))):
                        last = pe.matmul(xg[:, k * EA:(k + 1) * EA], l[:, k * P:(k + 1) * P], r[:, :], start=n == 0, stop=n == 2)
                last.then_inc(e_gate, 1)

            def hidden(i, e):
                if e == 0:
                    pe.wait_ge(v_x1l, i + 1)
                for n in range(HC + 1):
                    q = (i * EA + e) * (HC + 1) + n
                    pe.wait_ge(v_hf, past(q - 2))
                    cols = (n * P, (HC + n) * P) if n < HC else (2 * HC * P,)
                    for which, c in enumerate(cols):
                        ws = slice(e * WC + c, e * WC + c + P)
                        o = hbank(n, which)
                        for m, (l, r) in enumerate(((wallh, x1h), (wallh, x1l), (walll, x1h))):
                            last = pe.matmul(o, l[:, ws], r[:, :], start=m == 0, stop=m == 2)
                    last.then_inc(e_h, 1)

            def down(i, e):
                q = i * EA + e
                pe.wait_ge(v_hl, (q + 1) * (HC + 1))
                pe.wait_ge(a_hh, (q + 1) * (HC + 1))
                pe.wait_ge(v_y, past(q))
                for k in range(TB):
                    cols = slice(k * P, (k + 1) * P)
                    for n in range(HC + 1):
                        rows = slice(0, P if n < HC else HT)
                        c = EA * WC + e * W2C + n * D
                        for m, (l, r) in enumerate(((hh, wallh), (hh, walll), (hl, wallh))):
                            last = pe.matmul(y[:, cols], l[rows, e % 2, n, cols], r[rows, c:c + D],
                                             start=n == 0 and m == 0, stop=n == HC and m == 2)
                last.then_inc(e_y, 1)

            def tile(i):
                hidden(i, 0)
                if not isinstance(i, int) or i > 0:
                    down(i - 1, EA - 1)
                gate_logits(i)
                for e in range(1, EA):
                    hidden(i, e)
                    if e == EA - 1 and (not isinstance(i, int) or i < NT - 1):
                        transpose_x1(i + 1)
                    down(i, e - 1)

            transpose_x1(0)
            tile(0)
            with pe.Fori(1, NT - 1) as i:
                tile(i)
            tile(NT - 1)
            down(NT - 1, EA - 1)

        @block.scalar
        def _(act):
            def exp_unit(b, par, a):
                t = b * UB + a
                k = UB * par + a
                act.wait_ge(e_tscores, t + 1)
                act.wait_ge(g_pl, past(t - 1))
                act.wait_ge(e_pv, past(t - 3))
                act.activation(p32[:, k % 2, :], ps_t[:, :], ACT.Exp, scale=SCALE).then_inc(a_p32, 1)
                act.activation(ph[:, k % 4, :], ps_t[:, :], ACT.Exp, scale=SCALE).then_inc(a_ph, 1)

            def body(b, par):
                for a in range(UB):
                    if a == 0 and has(b, 1) and has(b, 0):
                        act.wait_ge(e_xt, b + 2)
                        act.wait_ge(e_q, past(b + 1))
                        act.copy(xth[:, W:], ps_x).then_inc(a_xh, 1)
                    if a == 0 and has(b, 2):
                        act.wait_ge(ld_x, (b + 3) * 16)
                        act.dma_start(xst[:, :, :], xr[:, bass.ds((b + 2) * HB, HB), :]).then_inc(ld_xst, 16)
                    if a == 1 and has(b, 1):
                        act.wait_ge(e_k, b + 2)
                        act.wait_ge(v_km, past(b + 1))
                        act.copy(kh[:, :], ps_k).then_inc(a_kh, 1)
                        act.wait_ge(e_v, b + 2)
                        act.wait_ge(e_pv, past(b * UB))
                        act.copy(vaug[:, 1 - par, :, :, 0:DH], ps_v.rearrange("p (a g d) -> p a g d", a=UB, g=NG)).then_inc(a_vh, 1)
                    if a % 2 == 1 and has(b, -1):
                        n = b * HB - HB + a // 2
                        act.wait_ge(e_ot, n + 1)
                        act.wait_ge(e_op, past(n))
                        act.copy(oth[:, :], ps_m[:, 0:P]).then_inc(a_oth, 1)
                    if a == 2 and has(b, 1):
                        act.wait_ge(e_q, b + 2)
                        act.wait_ge(v_qa, past(2 * b + 2))
                        act.copy(qh[:, :], ps_q).then_inc(a_qh, 1)
                    if has(b, 0):
                        exp_unit(b, par, a)
                    if a == 3 and has(b, 0):
                        if isinstance(b, int) and b == 0:
                            act.wait_ge(ld_big, 16 * N_BIG)
                        act.copy(wallh[:, bass.ds(b * WSTEP, WSTEP)], wall32[:, bass.ds(b * WSTEP, WSTEP)]).then_inc(a_w, 1)

            act.wait_ge(v_pad, 1)
            act.wait_ge(e_xt, 1)
            act.copy(xth[:, W:], ps_x).then_inc(a_xh, 1)
            pairs(act, body, 0, 0)
            act.wait_ge(v_stats, 1)
            act.sqrt(rs[:, 4, :], rs[:, 3, :]).then_inc(a_sq, 1)

            def tile(i):
                def groups(e):
                    for n in range(HC + 1):
                        q = (i * EA + e) * (HC + 1) + n
                        rows = slice(0, P if n < HC else HT)
                        act.wait_ge(e_h, q + 1)
                        act.wait_ge(v_hf, past(q - 2))
                        act.activation(sg[rows, n % 3, :], bank[n % 3][rows, 0:512], ACT.Silu).then_inc(a_silu, 1)
                        if n > 0:
                            hi(e, n - 1, q - 1)
                    hi(e, HC, q)

                def hi(e, n, q):
                    rows = slice(0, P if n < HC else HT)
                    act.wait_ge(v_hf, q + 1)
                    act.wait_ge(e_y, past(i * EA + e - 1))
                    act.copy(hh[rows, e % 2, n, :], hf[rows, n % 3, :]).then_inc(a_hh, 1)

                for e in range(EA):
                    groups(e)
                    if e == 1:
                        if not isinstance(i, int) or i > 0:
                            act.wait_ge(v_fv, past(i))
                            act.sqrt(fs[:, 4, :], fs[:, 3, :]).then_inc(a_fsq, 1)
                        act.wait_ge(v_gc, i * NGATE + 3)
                        act.activation(ex[:, :, :], ge[:, :, :], ACT.Exp).then_inc(a_ex, 1)
                    if e == EA - 1 and (not isinstance(i, int) or i < NT - 1):
                        x1_hi(i + 1)

            def x1_hi(i):
                act.wait_ge(e_x1, i + 1)
                act.wait_ge(e_h, i * EA * (HC + 1))
                act.wait_ge(e_gate, past(i))
                act.copy(x1h[:, :], bank[3][:, 512:1024]).then_inc(a_x1h, 1)

            x1_hi(0)
            tile(0)
            with act.Fori(1, NT - 1) as i:
                tile(i)
            tile(NT - 1)
            act.wait_ge(v_fv, past(NT))
            act.sqrt(fs[:, 4, :], fs[:, 3, :]).then_inc(a_fsq, 1)

        @block.vector
        def _(dve):
            links = [0]

            def link(ins):
                links[0] += 1
                ins.then_inc(v_chain, 1)
                dve.wait_ge(v_chain, links[0])

            for tile_, value in ((xth[:, 0:W], 0.0), (xtl[:, 0:W], 0.0), (kbd[:, :, :, :], 0.0), (mx[:, :, :, :, :], 0.0),
                                 (onesh[:, :], 1.0), (vaug[:, :, :, :, 2 * DH:VC], 1.0), (wqh[:, :, :, :, :], 0.0),
                                 (wql[:, :, :, :, :], 0.0), (wkh[:, :, :, :], 0.0), (wkl[:, :, :, :], 0.0), (bqr[:, :, :, :, :], 0.0),
                                 (bkr[:, :, :, :], 0.0), (bvr[:, :], 0.0), (bor[:, :], 0.0)):
                last = dve.memset(tile_, value)
            link(last)
            dve.engine_nop().then_inc(v_pad, 1)
            dve.wait_ge(ld_cst, 16)
            dve.tensor_copy(identb[:, :], cst[:, C_ID:C_ID + P])
            dve.tensor_scalar(nidentb[:, :], cst[:, C_ID:C_ID + P], -1.0, None, ALU.mult)
            for n, at in enumerate((C_MS, C_MS0)):
                dve.tensor_copy(mask_s[:, n, :, :], cst[:, at:at + KW].unsqueeze(1).broadcast_to([P, NG, KW]))
            dve.wait_ge(a_xh, 1)
            dve.tensor_tensor(xtl[:, W:], ps_x, xth[:, W:], ALU.subtract).then_inc(v_xl, 1)
            for n, at in enumerate((C_MT, C_MT0)):
                dve.tensor_copy(mask_t[:, n, :, :], cst[:, at:at + W].unsqueeze(1).broadcast_to([P, 8, W]))
            dve.wait_ge(ld_small, 16 * N_SMALL)
            dve.tensor_copy(woh[:, :, :], wo32[:, :, :])
            dve.tensor_copy(gh[:, :], g32[:, :])
            dve.tensor_copy(biash[:, :], bias32[:, :])
            link(dve.tensor_copy(wqkvh[:, :], wqkv32[:, :]))
            dve.tensor_tensor(wqkvl[:, :], wqkv32[:, :], wqkvh[:, :], ALU.subtract)
            dve.tensor_tensor(wol[:, :, :], wo32[:, :, :], woh[:, :, :], ALU.subtract)
            dve.tensor_tensor(gl[:, :], g32[:, :], gh[:, :], ALU.subtract)
            link(dve.scalar_tensor_tensor(biasm[:, :], biash[:, :], cst[0:2, C_N1:C_N1 + 1], bias32[:, :], ALU.mult, ALU.add))
            for slot in range(1, SLOTS):
                for r in range(R):
                    for dst, src in ((wqh, wqkvh), (wql, wqkvl)):
                        dve.tensor_copy(dst[:, r, :, slot, :], src[:, 0:D].rearrange("p (g r d) -> p g r d", g=NG, r=R)[:, :, r, :])
                    dve.tensor_copy(bqr[0:2, r, :, slot, :], biasm[:, 0:D].rearrange("p (g r d) -> p g r d", g=NG, r=R)[:, :, r, :])
                for dst, src in ((wkh, wqkvh), (wkl, wqkvl)):
                    dve.tensor_copy(dst[:, :, slot, :], src[:, D:D + 32].rearrange("p (g d) -> p g d", g=NG))
                dve.tensor_copy(bkr[0:2, :, slot, :], biasm[:, D:D + 32].rearrange("p (g d) -> p g d", g=NG))
            dve.memset(bkr[0:1, :, 0, 0:1], 1.0)
            dve.tensor_copy(bvr[0:2, :], biasm[:, D + 32:D + 64])
            link(dve.tensor_copy(bor[0:2, :], biasm[:, D + 64:]))
            dve.engine_nop().then_inc(setup, 1)

            def mix_q(par, j):
                dve.scalar_tensor_tensor(qa[:, par, 2 * j:2 * j + 2, :, :].rearrange("p a r q -> p (a r q)"), qh[:, j * 512:(j + 1) * 512],
                                         cst[:, C_NQ:C_NQ + 1], ps_q[:, j * 512:(j + 1) * 512], ALU.mult, ALU.add).then_inc(v_qa, 1)

            def body(b, par):
                for a in range(UB):
                    t = b * UB + a
                    k = UB * par + a
                    nxt = (a < UB - 1 and has(b, 0)) or (a == UB - 1 and has(b, 1))
                    if a % 2 == 0 and has(b, -1):
                        m = b * HB - HB + a // 2
                        dve.wait_ge(e_pv, (m + 1) * 2)
                        o = ps_o.rearrange("p (n c) -> p n c", c=VC)
                        dve.reciprocal(rden[:, :], o[:, :, 2 * DH]).then_inc(v_rden, 1)
                        dve.wait_ge(v_rden, m + 1)
                        dve.wait_ge(g_o, past(m))
                        dve.tensor_tensor(ot2[:, :, :], o[:, :, 0:2 * DH], rden[:, :].unsqueeze(2).broadcast_to([P, 16, 2 * DH]), ALU.mult).then_inc(v_o, 1)
                    if nxt:
                        dve.wait_ge(e_scores, t + 2)
                        dve.tensor_reduce(mx[:, (k + 1) % 2, :, :, 0], ps_s[:, :].rearrange("p (r g k) -> p r g k", r=2, g=NG),
                                          AX.X, ALU.max).then_inc(v_mx, 1)
                    n = b * HB - HB - (a == 0)
                    add = (a == 2 and has(b, -1)) or (a == 0 and has(b, -2))
                    if add:
                        dve.wait_ge(e_op, n + 1)
                        dve.tensor_tensor(xr[:, bass.ds(n, 1), :], ps_m[:, 0:D].unsqueeze(1), xr[:, bass.ds(n, 1), :], ALU.add).then_inc(v_r, 1)
                    if a == 0 and has(b, 1) and has(b, 0):
                        dve.wait_ge(a_xh, b + 2)
                        dve.tensor_tensor(xtl[:, W:], ps_x, xth[:, W:], ALU.subtract).then_inc(v_xl, 1)
                    if a % 2 == 1 and has(b, -1):
                        dve.wait_ge(a_oth, b * HB - HB + a // 2 + 1)
                        dve.tensor_tensor(otl[:, :], ps_m[:, 0:P], oth[:, :], ALU.subtract).then_inc(v_otl, 1)
                    if a == 1 and has(b, 1):
                        dve.wait_ge(a_kh, b + 2)
                        dve.wait_ge(v_kbd, past(b + 1))
                        dve.scalar_tensor_tensor(km[:, :], kh[:, :], cst[:, C_NK:C_NK + 1], ps_k, ALU.mult, ALU.add).then_inc(v_km, 1)
                        dve.wait_ge(a_vh, b + 2)
                        dve.tensor_tensor(vaug[:, 1 - par, :, :, DH:2 * DH], ps_v.rearrange("p (a g d) -> p a g d", a=UB, g=NG),
                                          vaug[:, 1 - par, :, :, 0:DH], ALU.subtract).then_inc(v_vl, 1)
                        dve.wait_ge(v_km, b + 2)
                        dve.wait_ge(e_tscores, past(b * UB))
                        for g in range(NG):
                            rows = slice(g * 32, (g + 1) * 32)
                            last = dve.tensor_copy(kbd[rows, 1 - par, g, W:], km[rows, :])
                        last.then_inc(v_kbd, 1)
                    if a == 2 and has(b, 1):
                        dve.wait_ge(a_qh, b + 2)
                        mix_q(1 - par, 0)
                    if add:
                        dve.wait_ge(v_r, n + 1)
                    if nxt:
                        dve.wait_ge(e_maxt, t + 2)
                        dve.wait_ge(e_tscores, past(t))
                        nb, na = (par, a + 1) if a < UB - 1 else (1 - par, 0)
                        if na % 2 == 0:
                            dve.wait_ge(v_qa, (b * 2 + 2) if na == 2 else (b * 2 + 3))
                        dve.tensor_tensor(qm[:, (k + 1) % 2, :, :], ps_m.rearrange("p (r q) -> p r q", r=R),
                                          qa[:, nb, na, :, :], ALU.add).then_inc(v_qm, 1)
                    if a == 3 and has(b, 1):
                        mix_q(1 - par, 1)
                    if add:
                        dve.bn_stats(stats[:, bass.ds(n, 1), :].rearrange("p o c -> p (o c)"),
                                     xr[:, bass.ds(n, 1), :].rearrange("p o d -> p (o d)")).then_inc(v_chain, 1)

            pairs(dve, body, 0, 0)

            dve.wait_ge(v_w, B)
            links[0] += NBLK
            dve.wait_ge(v_chain, links[0])

            t = rs
            link(dve.tensor_tensor(t[:, 1, :], stats[:, :, 1], stats[:, :, 4], ALU.subtract))
            link(dve.tensor_tensor(t[:, 0, :], stats[:, :, 1], stats[:, :, 4], ALU.add))
            link(dve.tensor_tensor(t[:, 2, :], t[:, 1, :], t[:, 1, :], ALU.mult))
            link(dve.tensor_tensor(t[:, 3, :], stats[:, :, 2], stats[:, :, 5], ALU.add))
            link(dve.scalar_tensor_tensor(t[:, 1, :], t[:, 2, :], D / 4.0, t[:, 3, :], ALU.mult, ALU.add))
            link(dve.tensor_scalar(t[:, 3, :], t[:, 1, :], 1.0 / D, EPS, ALU.mult, ALU.add))
            dve.engine_nop().then_inc(v_stats, 1)
            dve.wait_ge(a_sq, 1)
            link(dve.reciprocal(t[:, 5, :], t[:, 4, :]))
            link(dve.tensor_tensor(t[:, 1, :], t[:, 5, :], t[:, 5, :], ALU.mult))
            link(dve.tensor_tensor(t[:, 2, :], t[:, 1, :], t[:, 3, :], ALU.mult))
            link(dve.tensor_scalar(t[:, 1, :], t[:, 2, :], -0.5, 1.5, ALU.mult, ALU.add))
            link(dve.tensor_tensor(rstd[:, :], t[:, 5, :], t[:, 1, :], ALU.mult))
            link(dve.scalar_tensor_tensor(nmr[:, :], t[:, 0, :], -0.5, rstd[:, :], ALU.mult, ALU.mult))
            base = links[0]

            CH = TB + 1 + 8 + 3 + TB + 5 + 5

            def x1_norm(i, count):
                for k in range(TB):
                    blk = i * TB + k
                    last = dve.tensor_scalar(xr[:, bass.ds(blk, 1), :].rearrange("p o d -> p (o d)"), xr[:, bass.ds(blk, 1), :].rearrange("p o d -> p (o d)"),
                                             rstd[:, bass.ds(blk, 1)], nmr[:, bass.ds(blk, 1)], ALU.mult, ALU.add)
                    last.then_inc(v_x1n, 1)
                dve.wait_ge(v_x1n, (i + 1) * TB)
                dve.wait_ge(e_x1, past(i))
                dve.tensor_scalar(x1st[:, :, :], xr[:, bass.ds(i * TB, TB), :], 1.0, None, ALU.mult).then_inc(v_x1, 1)

            def x1_lo(i):
                dve.wait_ge(a_x1h, i + 1)
                dve.tensor_tensor(x1l[:, :], bank[3][:, 512:1024], x1h[:, :], ALU.subtract).then_inc(v_x1l, 1)

            def groups(i, e):
                def lo(n, q):
                    rows = slice(0, P if n < HC else HT)
                    dve.wait_ge(a_hh, q + 1)
                    dve.tensor_tensor(hl[rows, e % 2, n, :], hf[rows, n % 3, :], hh[rows, e % 2, n, :], ALU.subtract).then_inc(v_hl, 1)
                for n in range(HC + 1):
                    q = (i * EA + e) * (HC + 1) + n
                    rows = slice(0, P if n < HC else HT)
                    w3part = bank[n % 3][:, 512:1024] if n < HC else bank[n % 3][HT:P, 0:512]
                    dve.wait_ge(a_silu, q + 1)
                    dve.wait_ge(v_hl, past(q - 2))
                    dve.wait_ge(a_hh, past(q - 2))
                    dve.tensor_tensor(hf[rows, n % 3, :], w3part, sg[rows, n % 3, :], ALU.mult).then_inc(v_hf, 1)
                    if n > 0:
                        lo(n - 1, q - 1)
                lo(HC, q)

            def combine(i, e):
                dve.wait_ge(e_y, i * EA + e + 1)
                for k in range(TB):
                    blk = i * TB + k
                    to = yst[:, k, :] if e == EA - 1 else xr[:, bass.ds(blk, 1), :].rearrange("p o d -> p (o d)")
                    last = dve.scalar_tensor_tensor(to, bank[3][:, k * D:(k + 1) * D], cw[:, k, e:e + 1],
                                                    xr[:, bass.ds(blk, 1), :].rearrange("p o d -> p (o d)"), ALU.mult, ALU.add)
                last.then_inc(v_y, 1)

            class Chain:
                def __init__(self, s, i, ch, first):
                    self.s, self.i, self.ch, self.n = s, i, ch, first

                def __call__(self, ins):
                    self.n += 1
                    ins.then_inc(self.s, 1)
                    dve.wait_ge(self.s, self.i * self.ch + self.n)

            

            def gate_ranks(i):
                c = Chain(v_gc, i, NGATE, 0)
                dve.wait_ge(e_gate, i + 1)
                c(dve.tensor_copy(lg[:, :, :], bank[3][:, 512:512 + TB * EA].rearrange("p (k e) -> p k e", k=TB)))
                li = lg[:, :, :].unsqueeze(3).broadcast_to([P, TB, EA, EA])
                lj = lg[:, :, :].unsqueeze(2).broadcast_to([P, TB, EA, EA])
                tri = cst[:, C_TRI:C_TRI + EA * EA].rearrange("p (a b) -> p a b", a=EA).unsqueeze(1).broadcast_to([P, TB, EA, EA])
                c(dve.tensor_reduce(gm[:, :], lg[:, :, :], AX.X, ALU.max))
                c(dve.tensor_tensor(ge[:, :, :], lg[:, :, :], gm[:, :].unsqueeze(2).broadcast_to([P, TB, EA]), ALU.subtract))
                c(dve.tensor_tensor(gt[:, :, :, :], lj, li, ALU.is_gt))
                c(dve.tensor_tensor(eq[:, :, :, :], lj, li, ALU.is_equal))
                c(dve.tensor_tensor(eq[:, :, :, :], eq[:, :, :, :], tri, ALU.mult))
                c(dve.tensor_tensor(gt[:, :, :, :], gt[:, :, :, :], eq[:, :, :, :], ALU.add))
                c(dve.tensor_reduce(rank[:, :, :], gt[:, :, :, :], AX.X, ALU.add))

            def gate_weights(i):
                c = Chain(v_gc, i, NGATE, 8)
                dve.wait_ge(a_ex, i + 1)
                c(dve.scalar_tensor_tensor(cwu[:, :, :], rank[:, :, :], TOPK - 0.5, ex[:, :, :], ALU.is_lt, ALU.mult))
                c(dve.tensor_reduce(gs[:, :], cwu[:, :, :], AX.X, ALU.add))
                c(dve.reciprocal(gr[:, :], gs[:, :]))
                c(dve.tensor_tensor(cw[:, :, :], cwu[:, :, :], gr[:, :].unsqueeze(2).broadcast_to([P, TB, EA]), ALU.mult))
                assert c.n == NGATE

            def moments(i):
                c = Chain(v_fc, i, NFIN, 0)
                dve.wait_ge(v_y, (i + 1) * EA)
                for k in range(TB):
                    last = dve.bn_stats(fst[:, k, :], yst[:, k, :])
                c(last)
                c(dve.tensor_tensor(fs[:, 1, :], fst[:, :, 1], fst[:, :, 4], ALU.subtract))
                c(dve.tensor_tensor(fs[:, 0, :], fst[:, :, 1], fst[:, :, 4], ALU.add))
                c(dve.tensor_tensor(fs[:, 2, :], fs[:, 1, :], fs[:, 1, :], ALU.mult))
                c(dve.tensor_tensor(fs[:, 5, :], fst[:, :, 2], fst[:, :, 5], ALU.add))
                c(dve.scalar_tensor_tensor(fs[:, 1, :], fs[:, 2, :], D / 4.0, fs[:, 5, :], ALU.mult, ALU.add))
                dve.tensor_scalar(fs[:, 3, :], fs[:, 1, :], 1.0 / D, EPS, ALU.mult, ALU.add).then_inc(v_fv, 1)

            def final(i):
                c = Chain(v_fc, i, NFIN, 6)
                dve.wait_ge(a_fsq, i + 1)
                c(dve.reciprocal(fs[:, 5, :], fs[:, 4, :]))
                c(dve.tensor_tensor(fs[:, 1, :], fs[:, 5, :], fs[:, 5, :], ALU.mult))
                c(dve.tensor_tensor(fs[:, 2, :], fs[:, 1, :], fs[:, 3, :], ALU.mult))
                c(dve.tensor_scalar(fs[:, 1, :], fs[:, 2, :], -0.5, 1.5, ALU.mult, ALU.add))
                c(dve.tensor_tensor(frs[:, :], fs[:, 5, :], fs[:, 1, :], ALU.mult))
                c(dve.scalar_tensor_tensor(fnm[:, :], fs[:, 0, :], -0.5, frs[:, :], ALU.mult, ALU.mult))
                assert c.n == NFIN
                dve.wait_ge(st_out, past(i * 16))
                for k in range(TB):
                    last = dve.tensor_scalar(ost[:, k, :], yst[:, k, :], frs[:, k:k + 1], fnm[:, k:k + 1], ALU.mult, ALU.add)
                last.then_inc(v_out, 1)

            def tile(i):
                inner = not isinstance(i, int)
                groups(i, 0)
                if inner or i > 0:
                    combine(i - 1, EA - 1)
                    moments(i - 1)
                gate_ranks(i)
                for e in range(1, EA):
                    groups(i, e)
                    if e == 1:
                        if inner or i > 0:
                            final(i - 1)
                        gate_weights(i)
                    if e == 2 and (inner or i < NT - 1):
                        x1_norm(i + 1, 0)
                    if e == EA - 1 and (inner or i < NT - 1):
                        x1_lo(i + 1)
                    combine(i, e - 1)

            x1_norm(0, 0)
            x1_lo(0)
            tile(0)
            with dve.Fori(1, NT - 1) as i:
                tile(i)
            tile(NT - 1)
            combine(NT - 1, EA - 1)
            moments(NT - 1)
            final(NT - 1)


def constants():
    import numpy as np
    c = np.zeros((P, C_ALL), np.float32)
    c[:, C_ID:C_ID + P] = np.eye(P)
    q = np.arange(P)[:, None] % W
    key = np.arange(KW)[None, :]
    seen = (key > q) & (key <= W + q)
    c[:, C_MS:C_MS + KW] = np.where(seen, 0, -1e30)
    c[:, C_MS0:C_MS0 + KW] = np.where(seen & (key >= W), 0, -1e30)
    c[:, C_MT:C_MT + W] = c[0:W, C_MS:C_MS + KW].T
    c[:, C_MT0:C_MT0 + W] = c[0:W, C_MS0:C_MS0 + KW].T
    slot = np.arange(P) % 32 // DH
    c[:, C_NQ] = -1.0 * (slot == 2)
    c[:, C_NK] = -1.0 * (slot == 3)
    c[1, C_N1] = -1.0
    i, j = np.arange(EA)[:, None], np.arange(EA)[None, :]
    c[:, C_TRI:] = (j < i).astype(np.float32).reshape(-1)
    return c


def kernel(L0_attn_x, L0_attn_Wq, L0_attn_bq, L0_attn_Wk, L0_attn_bk, L0_attn_Wv, L0_attn_bv, L0_attn_Wo, L0_attn_bo,
           L0_ffn_gate_w, L0_ffn_w1, L0_ffn_w2, L0_ffn_w3):
    import numpy as np
    import concourse.bacc as bacc
    from concourse.bass_utils import run_bass_kernel_spmd

    nc = bacc.Bacc("TRN2", target_bir_lowering=False, num_devices=1)
    named = {"x": L0_attn_x, "wq": L0_attn_Wq, "bq": L0_attn_bq, "wk": L0_attn_Wk, "bk": L0_attn_bk, "wv": L0_attn_Wv,
             "bv": L0_attn_bv, "wo": L0_attn_Wo, "bo": L0_attn_bo, "gate": L0_ffn_gate_w, "w1": L0_ffn_w1, "w2": L0_ffn_w2,
             "w3": L0_ffn_w3, "const": constants()}
    arrays, args = {}, []
    for name, a in named.items():
        a = np.ascontiguousarray(a)
        arrays[f"in_{name}"] = a
        args.append(nc.dram_tensor(f"in_{name}", a.shape, mybir.dt.from_np(a.dtype), kind="ExternalInput").ap())
    o = nc.dram_tensor("out", (NBLK, P, D), F32, kind="ExternalOutput").ap()
    build(nc, *args, o)
    r = run_bass_kernel_spmd(nc, [arrays], core_ids=[0])
    return r.results[0]["out"].reshape(B, S, D)
```

```python
from contextlib import ExitStack

import concourse.bass as bass
from concourse import mybir

F32 = mybir.dt.float32
F16 = mybir.dt.float16
BF16 = mybir.dt.bfloat16
ALU = mybir.AluOpType
ACT = mybir.ActivationFunctionType
AX = mybir.AxisListType

P = 128
B, S, D = 32, 256, 128
NH, NG, DH = 16, 4, 8
R = NH // NG
W = 64
UB = S // W
KW = 2 * W
HB = S // P
NBLK = B * HB
SLOTS = 4
VC = 2 * DH + 1
E, EA, TOPK = 8, 4, 2
H = 704
HC = H // P
HT = H - HC * P
WC = 2 * H
W2C = (HC + 1) * D
WALL = EA * (WC + W2C)
WSTEP = WALL // B
TB = 4
TT = TB * P
LO_POOL = (1, 4)
LO_DVE = (0, 2, 3, 5)
NGATE, NFIN = 10, 11
NT = NBLK // TB
LOOP = 4
SCALE = float(DH) ** -0.5
EPS = 1e-5
C_ID, C_MS, C_MS0, C_MT, C_MT0, C_SQ, C_SK, C_N1, C_TRI = 0, 128, 256, 384, 448, 512, 513, 514, 515
C_ALL = C_TRI + EA * EA
assert (B - 4) % LOOP == 0 and LOOP % 2 == 0 and WALL % B == 0 and HT * 2 == P


def build(nc, x, wq, bq, wk, bk, wv, bv, wo, bo, gate, w1, w2, w3, const, out):
    ctx = ExitStack()
    with ctx:
        def sb(name, shape, dt):
            return ctx.enter_context(nc.sbuf_tensor(name, shape, dt))

        def pb(name, shape, dt=F32):
            return ctx.enter_context(nc.psum_tensor(name, shape, dt))

        def sem(name):
            return ctx.enter_context(nc.semaphore(name))

        xr = sb("xr", [P, NBLK, D], F32)
        stats = sb("stats", [P, NBLK, 6], F32)
        wall32 = sb("wall32", [P, WALL], F32)
        wallh = sb("wallh", [P, WALL], F16)
        walll = sb("walll", [P, WALL], F16)
        cst = sb("cst", [P, C_ALL], F32)
        identb = sb("identb", [P, P], BF16)
        nidentb = sb("nidentb", [P, P], BF16)
        onesh = sb("onesh", [P, S], F16)
        mask_s = sb("mask_s", [P, 2, NG, KW], BF16)
        mask_t = sb("mask_t", [P, 2, 8, W], BF16)
        wqkv32 = sb("wqkv32", [P, D + 2 * NG * DH], F32)
        wqkvh = sb("wqkvh", [P, D + 2 * NG * DH], F16)
        wqkvl = sb("wqkvl", [P, D + 2 * NG * DH], F16)
        wqh = sb("wqh", [P, R, NG, SLOTS, DH], F16)
        wql = sb("wql", [P, R, NG, SLOTS, DH], F16)
        wkh = sb("wkh", [P, NG, SLOTS, DH], F16)
        wkl = sb("wkl", [P, NG, SLOTS, DH], F16)
        wo32 = sb("wo32", [P, 2, D], F32)
        woh = sb("woh", [P, 2, D], F16)
        wol = sb("wol", [P, 2, D], F16)
        bias32 = sb("bias32", [2, 2 * D + 2 * NG * DH], F32)
        biash = sb("biash", [2, 2 * D + 2 * NG * DH], F16)
        biasm = sb("biasm", [2, 2 * D + 2 * NG * DH], F16)
        bqr = sb("bqr", [P, R, NG, SLOTS, DH], F16)
        bkr = sb("bkr", [P, NG, SLOTS, DH], F16)
        bcol = sb("bcol", [P, R + 1], F32)
        bcolm = sb("bcolm", [P, R + 1], F32)
        bvr = sb("bvr", [P, NG * DH], F16)
        bor = sb("bor", [P, D], F16)
        g32 = sb("g32", [P, EA], F32)
        gh = sb("gh", [P, EA], F16)
        gl = sb("gl", [P, EA], F16)
        xst = sb("xst", [P, HB, D], F32)
        xth = sb("xth", [P, W + S], F16)
        xtl = sb("xtl", [P, W + S], F16)
        qh = sb("qh", [P, R * S], F16)
        qa = sb("qa", [P, 2, UB, R, W], F16)
        kh = sb("kh", [P, S], F16)
        km = sb("km", [P, S], F16)
        kbd = sb("kbd", [P, 2, NG, W + S], F16)
        vaug = sb("vaug", [P, 2, UB, NG, VC], F16)
        mx = sb("mx", [P, 2, 2, NG, 32], BF16)
        qm = sb("qm", [P, 2, R, W], F16)
        p32 = sb("p32", [P, 2, NH * W], F32)
        ph = sb("ph", [P, 4, NH * W], F16)
        pl = sb("pl", [P, 4, NH * W], F16)
        rden = sb("rden", [P, 2 * 8], F32)
        ot2 = sb("ot2", [P, 2 * 8, 2 * DH], F32)
        o32 = sb("o32", [P, 2 * 8, DH], F32)
        oth = sb("oth", [P, P], F16)
        otl = sb("otl", [P, P], F16)
        rs = sb("rs", [P, 6, NBLK], F32)
        rstd = sb("rstd", [P, NBLK], F32)
        nmr = sb("nmr", [P, NBLK], F32)
        x1st = sb("x1st", [P, TB, D], F32)
        x1h = sb("x1h", [P, TT], F16)
        x1l = sb("x1l", [P, TT], F16)
        sg = sb("sg", [P, 3, TT], F32)
        hf = sb("hf", [P, 3, TT], F32)
        nh = (HC + 1) * TT
        hh, hl = (wall32[:, n * nh:(n + 1) * nh].bitcast(F16).rearrange("p (b c t) -> p b c t", b=2, c=HC + 1) for n in range(2))
        gt = sb("gt", [P, TB, EA, EA], F32)
        eq = sb("eq", [P, TB, EA, EA], F32)
        rank = sb("rank", [P, TB, EA], F32)
        gm = sb("gm", [P, TB], F32)
        ge = sb("ge", [P, TB, EA], F32)
        ex = sb("ex", [P, TB, EA], F32)
        cwu = sb("cwu", [P, TB, EA], F32)
        gs = sb("gs", [P, TB], F32)
        gr = sb("gr", [P, TB], F32)
        cw = sb("cw", [P, TB, EA], F32)
        silu_in = sb("silu_in", [P, 2], F32)
        fst = sb("fst", [P, TB, 6], F32)
        fs = sb("fs", [P, 6, TB], F32)
        frs = sb("frs", [P, TB], F32)
        fnm = sb("fnm", [P, TB], F32)
        yst = sb("yst", [P, TB, D], F32)
        ost = sb("ost", [P, TB, D], F32)
        bank = [pb(f"bank{i}", [P, 1024]) for i in range(4)]
        ps_s, ps_t = bank[0], bank[1]
        b45, b67 = bank[2], bank[3]
        ps_m = b45[:, 0:R * W]
        ps_o = b45[:, 512:512 + 2 * 8 * VC]
        ps_x, ps_k, ps_v, ps_q = b67[:, 0:S], b67[:, 0:S], b67[:, 512:512 + UB * NG * DH], b67[:, :]

        ld_x = sem("ld_x")
        ld_xst = sem("ld_xst")
        ld_cst = sem("ld_cst")
        ld_qkv = sem("ld_qkv")
        ld_small = sem("ld_small")
        setup_o = sem("setup_o")
        g_zero = sem("g_zero")
        v_pad = sem("v_pad")
        ld_big = sem("ld_big")
        st_out = sem("st_out")
        setup = sem("setup")
        e_scores, e_maxt, e_tscores, e_pv = sem("e_scores"), sem("e_maxt"), sem("e_tscores"), sem("e_pv")
        e_xt, e_k, e_q, e_v, e_ot, e_op = (sem(n) for n in ("e_xt", "e_k", "e_q", "e_v", "e_ot", "e_op"))
        a_xh, a_kh, a_qh, a_vh, a_oth, a_p32, a_ph, a_w = (
            sem(n) for n in ("a_xh", "a_kh", "a_qh", "a_vh", "a_oth", "a_p32", "a_ph", "a_w"))
        v_xl, v_km, v_kbd, v_qa, v_vl, v_mx, v_qm, v_rden, v_o, v_otl, v_r = (
            sem(n) for n in ("v_xl", "v_km", "v_kbd", "v_qa", "v_vl", "v_mx", "v_qm", "v_rden",
                             "v_o", "v_otl", "v_r"))
        g_pl, g_o, g_w = sem("g_pl"), sem("g_o"), sem("g_w")
        e_bias, v_bias = sem("e_bias"), sem("v_bias")
        v_st = sem("v_st")
        v_chain = sem("v_chain")
        v_stats, v_gc, v_fc = (sem(n) for n in ("v_stats", "v_gc", "v_fc"))
        a_sq = sem("a_sq")
        e_x1, e_gate, e_h, e_y = sem("e_x1"), sem("e_gate"), sem("e_h"), sem("e_y")
        a_x1h, a_silu, a_hh, a_ex, a_fsq = (sem(n) for n in ("a_x1h", "a_silu", "a_hh", "a_ex", "a_fsq"))
        g_hl = sem("g_hl")
        v_x1, v_x1l, v_hf, v_hl, v_y, v_fv = (
            sem(n) for n in ("v_x1", "v_x1l", "v_hf", "v_hl", "v_y", "v_fv"))
        a_out = sem("a_out")

        def past(n):
            return max(n, 0) if isinstance(n, int) else n

        block = ctx.enter_context(nc.Block())

        def elements(eng, body):
            for b in (-1, 0, 1):
                body(b, b % 2)
            with eng.Fori(0, (B - 4) // LOOP) as i:
                for k in range(LOOP):
                    body(i * LOOP + 2 + k, k % 2)
            for b in (B - 2, B - 1, B, B + 1):
                body(b, b % 2)

        def tail(b):
            return isinstance(b, int) and b == B

        def has(b, k):
            return not isinstance(b, int) or 0 <= b + k < B

        @block.sync
        def _(sp):
            sp.dma_start(xst[:, :, :], x[0].rearrange("(h p) d -> p h d", p=P)).then_inc(ld_xst, 16)
            sp.dma_start(cst[:, :], const).then_inc(ld_cst, 16)
            for at, n, bias in ((0, D, bq), (D, 32, bk), (D + 32, 32, bv), (D + 64, D, bo)):
                sp.dma_start(bias32[:, at:at + n], bias.unsqueeze(0).broadcast_to([2, n])).then_inc(ld_qkv, 16)
            sp.dma_start(xr[:, 0:HB, :], x[0].rearrange("(h p) d -> p h d", p=P)).then_inc(ld_x, 16)
            sp.dma_start(xr[:, HB:2 * HB, :], x[1].rearrange("(h p) d -> p h d", p=P)).then_inc(ld_x, 16)
            for half in range(2):
                for r1 in range(2):
                    sp.dma_start(wo32[half * 64:(half + 1) * 64, r1, :],
                                 wo.rearrange("(m r d) n -> r m d n", r=2, d=DH)[r1]).then_inc(ld_small, 16)
            sp.dma_start(g32[:, :], gate[0:EA, :].rearrange("e d -> d e"), allow_slow_non_contiguous=True).then_inc(ld_small, 16)
            for e in range(EA):
                c = e * WC
                sp.dma_start(wall32[:, c:c + HC * P], w1[e, :, 0:HC * P]).then_inc(ld_big, 16)
                sp.dma_start(wall32[:, c + HC * P:c + 2 * HC * P], w3[e, :, 0:HC * P]).then_inc(ld_big, 16)
                sp.dma_start(wall32[:, c + 2 * HC * P:c + 2 * HC * P + HT], w1[e, :, HC * P:H]).then_inc(ld_big, 16)
                sp.dma_start(wall32[:, c + 2 * HC * P + HT:c + WC], w3[e, :, HC * P:H]).then_inc(ld_big, 16)
                c = EA * WC + e * W2C
                sp.dma_start(wall32[:, c:c + HC * D].rearrange("p (k d) -> p k d", k=HC),
                             w2[e, 0:HC * P, :].rearrange("(k p) d -> p k d", p=P)).then_inc(ld_big, 16)
                for half in range(2):
                    sp.dma_start(wall32[half * HT:(half + 1) * HT, c + HC * D:c + W2C], w2[e, HC * P:H, :]).then_inc(ld_big, 16)
                b = 2 + e
                sp.wait_ge(ld_x, b * 16)
                sp.dma_start(xr[:, b * HB:b * HB + HB, :], x[b].rearrange("(h p) d -> p h d", p=P)).then_inc(ld_x, 16)
            with sp.Fori(2 + EA, B) as b:
                sp.wait_ge(ld_x, b * 16)
                sp.dma_start(xr[:, bass.ds(b * HB, HB), :],
                             x[bass.ds(b, 1)].rearrange("o (h p) d -> p (o h) d", p=P)).then_inc(ld_x, 16)
            with sp.Fori(1, NT + 1) as i:
                sp.wait_ge(a_out, i)
                sp.dma_start(out[bass.ds(i * TB - TB, TB)].rearrange("k p d -> p k d"), ost[:, :, :]).then_inc(st_out, 16)
            sp.wait_ge(st_out, 16 * NT)

        N_QKV, N_SMALL = 3 + 4, 4 + 1
        N_BIG = EA * 7

        @block.gpsimd
        def _(pool):
            for tile_, value in ((bqr[:, :, :, :, :], 0.0), (bkr[:, :, :, :], 0.0), (wqh[:, :, :, :, :], 0.0), (wql[:, :, :, :, :], 0.0),
                                 (wkh[:, :, :, :], 0.0), (wkl[:, :, :, :], 0.0), (bvr[:, :], 0.0), (bor[:, :], 0.0),
                                 (mx[:, :, :, :, :], 0.0), (kbd[:, :, :, :], 0.0), (vaug[:, :, :, :, 2 * DH:VC], 1.0)):
                last = pool.memset(tile_, value)
            last.then_inc(g_zero, 1)

            def body(b, par):
                def lo_part(t, k):
                    pool.wait_ge(a_ph, t + 1)
                    pool.wait_ge(e_pv, past(t - 3))
                    pool.tensor_tensor(pl[:, k % 4, :], p32[:, k % 2, :], ph[:, k % 4, :], ALU.subtract).then_inc(g_pl, 1)

                def sum_o(n):
                    pool.wait_ge(v_o, n + 1)
                    pool.wait_ge(e_ot, past(n))
                    pool.tensor_tensor(o32[:, :, :], ot2[:, :, 0:DH], ot2[:, :, DH:2 * DH], ALU.add).then_inc(g_o, 1)

                for s in range(UB):
                    if s in (0, 2) and has(b, -1):
                        sum_o(b * HB - HB + s // 2)
                    if s == 0 and has(b, -1):
                        pool.wait_ge(a_w, b)
                    if has(b, 0):
                        lo_part(b * UB + s, UB * par + s)
                    if s == 0 and has(b, -1):
                        share = bass.ds(b * WSTEP - WSTEP, WSTEP)
                        pool.tensor_tensor(walll[:, share], wall32[:, share], wallh[:, share], ALU.subtract).then_inc(g_w, 1)
            elements(pool, body)

            def hidden_lo(i):
                for e in range(EA):
                    for n in LO_POOL:
                        q = (i * EA + e) * (HC + 1) + n
                        pool.wait_ge(v_hf, q + 1)
                        pool.wait_ge(a_hh, q + 1)
                        pool.tensor_tensor(hl[:, e % 2, n, :], hf[:, n % 3, :], hh[:, e % 2, n, :], ALU.subtract).then_inc(g_hl, 1)

            with pool.Fori(0, NT) as i:
                hidden_lo(i)

        @block.tensor
        def _(pe):
            xg = bank[3][:, 512:1024]
            ident = cst[:, C_ID:C_ID + P]
            def transpose_x1(i):
                pe.wait_ge(v_x1, i + 1)
                pe.wait_ge(v_gc, past((i - 1) * NGATE + 2))
                for k in range(TB):
                    last = pe.transpose(xg[:, k * P:(k + 1) * P], x1st[:, k, :], ident)
                last.then_inc(e_x1, 1)

            def transpose_x(b):
                pe.wait_ge(ld_xst, 16 * b + 16)
                pe.wait_ge(v_qa, past(2 * b))
                for h in range(HB):
                    last = pe.transpose(ps_x[:, h * P:(h + 1) * P], xst[:, h, :], cst[:, C_ID:C_ID + P])
                last.then_inc(e_xt, 1)

            def project_k(b):
                pe.wait_ge(v_xl, b + 1)
                pe.wait_ge(a_xh, b + 1)
                for n, (w, m) in enumerate(((wkh, xth[:, W:]), (wkh, xtl[:, W:]), (wkl, xth[:, W:]))):
                    last = pe.matmul(ps_k, w[:, :, :, :].rearrange("p g s d -> p (g s d)"), m, start=n == 0, stop=n == 2)
                last.then_inc(e_k, 1)

            def project_q(b, j):
                if j == 0:
                    pe.wait_ge(v_km, b + 1)
                else:
                    pe.wait_ge(v_vl, past(b))
                for r in (2 * j, 2 * j + 1):
                    for n, (w, m) in enumerate(((wqh, xth), (wqh, xtl), (wql, xth))):
                        last = pe.matmul(ps_q[:, r * S:(r + 1) * S], w[:, r, :, :, :].rearrange("p g s d -> p (g s d)"), m[:, W:],
                                         start=n == 0, stop=n == 2)
                last.then_inc(e_q, 1)

            def project_v(b):
                pe.wait_ge(v_qa, 2 * b + 1)
                for a in range(UB):
                    o = ps_v[:, a * 32:(a + 1) * 32]
                    win = slice(a * W, a * W + KW)
                    for n, (l, r) in enumerate(((onesh[:, 0:P], bvr[:, :]), (xth[:, win], wqkvh[:, D + 32:]),
                                                (xtl[:, win], wqkvh[:, D + 32:]), (xth[:, win], wqkvl[:, D + 32:]))):
                        last = pe.matmul(o, l, r, start=n == 0, stop=n == 3)
                last.then_inc(e_v, 1)

            def scores(b, par, a):
                t = b * UB + a
                if a == 0:
                    pe.wait_ge(v_qa, b * 2 + 2)
                    pe.wait_ge(v_kbd, b + 1)
                pe.wait_ge(v_mx, past(t))
                for rp in range(2):
                    o = ps_s[:, rp * 512:(rp + 1) * 512]
                    pe.matmul(o, identb[:, :], mask_s[:, int(a == 0), :, :].rearrange("p g k -> p (g k)"), start=True, stop=False)
                    last = pe.matmul(o, qa[:, par, a, 2 * rp:2 * rp + 2, :].rearrange("p r q -> p (r q)"),
                                     kbd[:, par, :, a * W:a * W + KW], start=False, stop=True)
                last.then_inc(e_scores, 1)

            def max_rows(t, k):
                pe.wait_ge(v_mx, t + 1)
                pe.wait_ge(v_qm, past(t))
                for rp in range(2):
                    last = pe.matmul(ps_m[:, rp * P:(rp + 1) * P], mx[:, k % 2, rp, :, :].rearrange("p g c -> p (g c)"),
                                     nidentb[:, :], start=True, stop=True)
                last.then_inc(e_maxt, 1)

            def tscores(b, par, a):
                t = b * UB + a
                pe.wait_ge(v_qm, t + 1)
                pe.wait_ge(a_ph, past(t))
                for j in range(2):
                    o = ps_t[:, j * 512:(j + 1) * 512]
                    pe.matmul(o, identb[:, :], mask_t[:, int(a == 0), :, :].rearrange("p h q -> p (h q)"), start=True, stop=False)
                    for g in (2 * j, 2 * j + 1):
                        last = pe.matmul(ps_t[:, g * 256:(g + 1) * 256], kbd[:, par, g, a * W:a * W + KW],
                                         qm[:, a % 2, :, :].rearrange("p r q -> p (r q)"), start=False, stop=g % 2 == 1)
                last.then_inc(e_tscores, 1)

            def pv(b, par, a):
                t = b * UB + a
                pe.wait_ge(g_pl, t + 1)
                pe.wait_ge(a_ph, t + 1)
                pe.wait_ge(v_vl, b + 1)
                pe.wait_ge(v_o, past(b * HB + a // 2))
                k = (UB * par + a) % 4
                for g in range(NG):
                    for rp in range(2):
                        n = (a % 2) * 8 + g * 2 + rp
                        c = (g * 2 + rp) * P
                        pe.matmul(ps_o[:, n * VC:(n + 1) * VC], ph[:, k, c:c + P], vaug[:, par, a, g, :], start=True, stop=False)
                        last = pe.matmul(ps_o[:, n * VC:(n + 1) * VC], pl[:, k, c:c + P], vaug[:, par, a, g, :], start=False, stop=True)
                last.then_inc(e_pv, 1)

            def transpose_o(n):
                pe.wait_ge(g_o, n + 1)
                pe.wait_ge(v_r, past(n))
                pe.transpose(ps_m[:, 0:P], o32[:, :, :].rearrange("p a b -> p (a b)"), cst[:, C_ID:C_ID + P]).then_inc(e_ot, 1)

            def project_o(n):
                pe.wait_ge(v_otl, n + 1)
                pe.matmul(ps_m[:, 0:D], onesh[:, 0:P], bor[:, :], start=True, stop=True)
                for m, (l, r) in enumerate(((oth, woh), (otl, woh), (oth, wol))):
                    for r1 in range(2):
                        for u in range(2):
                            rows = slice(u * 64, (u + 1) * 64)
                            last = pe.matmul(ps_m[rows, 0:D], l[rows, r1 * 64:(r1 + 1) * 64], r[rows, r1, :],
                                             start=False, stop=m == 2 and r1 == 1, skip_group_check=True)
                last.then_inc(e_op, 1)

            def body(b, par):
                for a in range(UB):
                    t = b * UB + a
                    k = par * UB + a
                    if a < UB - 1 and has(b, 0):
                        scores(b, par, a + 1)
                    if a == UB - 1 and has(b, 1):
                        scores(b + 1, 1 - par, 0)
                    if a == 0 and has(b, 1):
                        project_k(b + 1)
                    if a < 2 and has(b, 1):
                        project_q(b + 1, 1 - a)
                    if a == 2 and has(b, 1):
                        project_v(b + 1)
                    if a == 3 and has(b, 2):
                        transpose_x(b + 2)
                    if a != 2 and has(b, 0) and (has(b, -1) if a else has(b, -2)):
                        pe.wait_ge(v_qm, t + 1)
                    if a % 2 == 1 and has(b, -1):
                        transpose_o(b * HB - HB + a // 2)
                    if a == 0 and has(b, -2):
                        project_o(b * HB - HB - 1)
                    if a == 0 and isinstance(b, int) and b == 1:
                        pe.wait_ge(setup_o, 1)
                    if a < 2 and has(b, -1):
                        pv(b - 1, 1 - par, a + 2)
                    if a >= 2 and has(b, 0):
                        pv(b, par, a - 2)
                    if a == 2 and tail(b):
                        transpose_x1(0)
                    if a == 2 and has(b, -1):
                        if has(b, 0):
                            pe.wait_ge(v_qm, t + 1)
                        project_o(b * HB - HB)
                    if has(b, 0):
                        tscores(b, par, a)
                    if (a < UB - 1 and has(b, 0)) or (a == UB - 1 and has(b, 1)):
                        if a % 2 == 1 and has(b, -1):
                            pe.wait_ge(v_otl, b * HB - HB + a // 2 + 1)
                        if a == 2 and has(b, -1):
                            pe.wait_ge(v_r, b * HB - HB + 1)
                        if a == 0 and has(b, -2):
                            pe.wait_ge(v_r, b * HB - HB)
                        max_rows(t + 1, k + 1)

            pe.wait_ge(ld_cst, 16)
            transpose_x(0)
            pe.wait_ge(setup, 1)
            for r in range(R + 1):
                w = (bqr[:, r, :, :, :] if r < R else bkr[:, :, :, :]).rearrange("p g s d -> p (g s d)")
                last = pe.matmul(b45[:, 512 + r:513 + r], w, onesh[:, 0:1], start=True, stop=True)
            last.then_inc(e_bias, 1)
            elements(pe, body)

            pe.wait_ge(g_w, B)
            b01, b23, b45_, b67_ = bank

            def hbank(n, which):
                return bank[n % 3][:, which * 512:(which + 1) * 512]

            y = bank[3][:, 0:512]

            def gate_logits(i):
                for k in range(TB):
                    for n, (l, r) in enumerate(((x1h, gh), (x1l, gh), (x1h, gl))):
                        last = pe.matmul(xg[:, k * EA:(k + 1) * EA], l[:, k * P:(k + 1) * P], r[:, :], start=n == 0, stop=n == 2)
                last.then_inc(e_gate, 1)

            def hidden(i, e):
                if e == 0:
                    pe.wait_ge(v_x1l, i + 1)
                for n in range(HC + 1):
                    q = (i * EA + e) * (HC + 1) + n
                    pe.wait_ge(v_hf, past(q - 2))
                    if isinstance(i, int) and i == 0 and e == 0 and n == 2:
                        pe.wait_ge(v_r, NBLK)
                    cols = (n * P, (HC + n) * P) if n < HC else (2 * HC * P,)
                    for which, c in enumerate(cols):
                        ws = slice(e * WC + c, e * WC + c + P)
                        o = hbank(n, which)
                        for m, (l, r) in enumerate(((wallh, x1h), (wallh, x1l), (walll, x1h))):
                            last = pe.matmul(o, l[:, ws], r[:, :], start=m == 0, stop=m == 2)
                    last.then_inc(e_h, 1)

            def down(i, e):
                q = i * EA + e
                pe.wait_ge(v_hl, (q + 1) * len(LO_DVE))
                pe.wait_ge(g_hl, (q + 1) * len(LO_POOL))
                pe.wait_ge(a_hh, (q + 1) * (HC + 1))
                pe.wait_ge(v_y, past(q))
                for k in range(TB):
                    cols = slice(k * P, (k + 1) * P)
                    for n in range(HC):
                        c = EA * WC + e * W2C + n * D
                        for m, (l, r) in enumerate(((hh, wallh), (hh, walll), (hl, wallh))):
                            pe.matmul(y[:, cols], l[:, e % 2, n, cols], r[:, c:c + D], start=n == 0 and m == 0, stop=False)
                    c = EA * WC + e * W2C + HC * D
                    pe.matmul(y[:, cols], hh[:, e % 2, HC, cols], wallh[:, c:c + D], start=False, stop=False)
                    last = pe.matmul(y[:, cols], hh[0:HT, e % 2, HC, cols], walll[0:HT, c:c + D], start=False, stop=True)
                last.then_inc(e_y, 1)

            def tile(i):
                hidden(i, 0)
                gate_logits(i)
                if not isinstance(i, int) or i > 0:
                    down(i - 1, EA - 1)
                for e in range(1, EA):
                    hidden(i, e)
                    if e == EA - 1 and (not isinstance(i, int) or i < NT - 1):
                        transpose_x1(i + 1)
                    down(i, e - 1)

            tile(0)
            with pe.Fori(1, NT - 1) as i:
                tile(i)
            tile(NT - 1)
            down(NT - 1, EA - 1)

        @block.scalar
        def _(act):
            def silu_table():
                act.activation(silu_in[:, 1:2], silu_in[:, 0:1], ACT.Silu)

            def x1_hi(i):
                act.wait_ge(e_x1, i + 1)
                act.wait_ge(e_h, i * EA * (HC + 1))
                act.wait_ge(e_gate, past(i))
                act.copy(x1h[:, :], bank[3][:, 512:1024]).then_inc(a_x1h, 1)

            def deviations(lo, hi):
                act.wait_ge(v_stats, 1 if lo == 0 else 2)
                act.sqrt(rs[:, 4, lo:hi], rs[:, 3, lo:hi]).then_inc(a_sq, 1)

            def exp_unit(b, par, a):
                t = b * UB + a
                k = UB * par + a
                act.wait_ge(e_tscores, t + 1)
                act.wait_ge(g_pl, past(t - 1))
                act.wait_ge(e_pv, past(t - 3))
                act.activation(p32[:, k % 2, :], ps_t[:, :], ACT.Exp, scale=SCALE).then_inc(a_p32, 1)
                act.activation(ph[:, k % 4, :], ps_t[:, :], ACT.Exp, scale=SCALE).then_inc(a_ph, 1)

            def hi_rows(to, v, c, r):
                return act.activation(to, v, ACT.Identity, scale=cst[:, c:c + 1], bias=bcolm[:, r:r + 1])

            def body(b, par):
                for a in range(UB):
                    if a == 0 and tail(b):
                        deviations(0, TB)
                    if a == 0 and has(b, 2):
                        act.wait_ge(e_xt, b + 2)
                        act.wait_ge(ld_x, (b + 3) * 16)
                        act.dma_start(xst[:, :, :], xr[:, bass.ds((b + 2) * HB, HB), :]).then_inc(ld_xst, 16)
                    if a % 2 == 1 and has(b, -1):
                        n = b * HB - HB + a // 2
                        act.wait_ge(e_ot, n + 1)
                        act.wait_ge(e_op, past(n))
                        act.copy(oth[:, :], ps_m[:, 0:P]).then_inc(a_oth, 1)
                    if a == 3 and tail(b):
                        x1_hi(0)
                    if a == 0 and has(b, 1):
                        act.wait_ge(e_k, b + 2)
                        act.wait_ge(v_km, past(b + 1))
                        hi_rows(kh[:, :], ps_k, C_SK, R).then_inc(a_kh, 1)
                    if a == 2 and has(b, 1):
                        act.wait_ge(e_v, b + 2)
                        act.wait_ge(e_pv, past(b * UB))
                        act.copy(vaug[:, 1 - par, :, :, 0:DH], ps_v.rearrange("p (a g d) -> p a g d", a=UB, g=NG)).then_inc(a_vh, 1)
                    if a < 2 and has(b, 1):
                        j = 1 - a
                        act.wait_ge(e_q, 2 * b + 3 + a)
                        act.wait_ge(v_qa, past(2 * b + 1 + a))
                        for r in (2 * j, 2 * j + 1):
                            last = hi_rows(qh[:, r * S:(r + 1) * S], ps_q[:, r * S:(r + 1) * S], C_SQ, r)
                        last.then_inc(a_qh, 1)
                    if a == 3 and has(b, 2):
                        act.wait_ge(e_xt, b + 3)
                        act.wait_ge(e_q, past(2 * b + 4))
                        act.copy(xth[:, W:], ps_x).then_inc(a_xh, 1)
                    if has(b, 0):
                        exp_unit(b, par, a)
                    if a == 3 and has(b, 0):
                        if isinstance(b, int) and b == 0:
                            act.wait_ge(ld_big, 16 * N_BIG)
                        act.copy(wallh[:, bass.ds(b * WSTEP, WSTEP)], wall32[:, bass.ds(b * WSTEP, WSTEP)]).then_inc(a_w, 1)

            act.dma_start(wqkv32[:, 0:D], wq).then_inc(ld_qkv, 16)
            act.dma_start(wqkv32[:, D:D + 32], wk).then_inc(ld_qkv, 16)
            act.dma_start(wqkv32[:, D + 32:D + 64], wv).then_inc(ld_qkv, 16)
            act.wait_ge(v_pad, 1)
            act.wait_ge(e_xt, 1)
            act.copy(xth[:, W:], ps_x).then_inc(a_xh, 1)
            act.wait_ge(v_bias, 1)
            elements(act, body)
            deviations(TB, NBLK)
            silu_table()

            def tile(i):
                def groups(e):
                    for n in range(HC + 1):
                        q = (i * EA + e) * (HC + 1) + n
                        rows = slice(0, P if n < HC else HT)
                        act.wait_ge(e_h, q + 1)
                        act.wait_ge(v_hf, past(q - 2))
                        act.activation(sg[rows, n % 3, :], bank[n % 3][rows, 0:512], ACT.Silu).then_inc(a_silu, 1)
                        if n > 0:
                            hi(e, n - 1, q - 1)
                    hi(e, HC, q)

                def hi(e, n, q):
                    rows = slice(0, P if n < HC else HT)
                    act.wait_ge(v_hf, q + 1)
                    act.wait_ge(e_y, past(i * EA + e - 1))
                    act.copy(hh[rows, e % 2, n, :], hf[rows, n % 3, :]).then_inc(a_hh, 1)

                for e in range(EA):
                    groups(e)
                    if e == 0:
                        act.wait_ge(v_gc, i * NGATE + 2)
                        act.activation(ex[:, :, :], ge[:, :, :], ACT.Exp).then_inc(a_ex, 1)
                        silu_table()
                    if e == 2 and (not isinstance(i, int) or i > 0):
                        act.wait_ge(v_fv, past(i))
                        act.sqrt(fs[:, 4, :], fs[:, 3, :]).then_inc(a_fsq, 1)
                        silu_table()
                    if e == EA - 1 and (not isinstance(i, int) or i < NT - 1):
                        x1_hi(i + 1)
                    if e == EA - 1 and (not isinstance(i, int) or i > 0):
                        final_norm(i - 1)

            def final_norm(i):
                act.wait_ge(v_fc, (i + 1) * NFIN)
                act.wait_ge(st_out, past(i * 16))
                for k in range(TB):
                    last = act.activation(ost[:, k, :], yst[:, k, :], ACT.Identity, scale=frs[:, k:k + 1], bias=fnm[:, k:k + 1])
                last.then_inc(a_out, 1)

            tile(0)
            with act.Fori(1, NT - 1) as i:
                tile(i)
            tile(NT - 1)
            act.wait_ge(v_fv, NT)
            act.sqrt(fs[:, 4, :], fs[:, 3, :]).then_inc(a_fsq, 1)
            final_norm(NT - 1)

        @block.vector
        def _(dve):
            links = [0]

            def link(ins):
                links[0] += 1
                ins.then_inc(v_chain, 1)
                dve.wait_ge(v_chain, links[0])

            for tile_, value in ((silu_in[:, :], 0.0), (xth[:, 0:W], 0.0), (xtl[:, 0:W], 0.0), (onesh[:, :], 1.0)):
                last = dve.memset(tile_, value)
            link(last)
            dve.engine_nop().then_inc(v_pad, 1)
            dve.wait_ge(ld_cst, 16)
            dve.tensor_copy(identb[:, :], cst[:, C_ID:C_ID + P])
            dve.tensor_scalar(nidentb[:, :], cst[:, C_ID:C_ID + P], -1.0, None, ALU.mult)
            for n, at in enumerate((C_MS, C_MS0)):
                dve.tensor_copy(mask_s[:, n, :, :], cst[:, at:at + KW].unsqueeze(1).broadcast_to([P, NG, KW]))
            dve.wait_ge(ld_qkv, 16 * N_QKV)
            dve.tensor_copy(biash[:, :], bias32[:, :])
            link(dve.tensor_copy(wqkvh[:, :], wqkv32[:, :]))
            dve.tensor_tensor(wqkvl[:, :], wqkv32[:, :], wqkvh[:, :], ALU.subtract)
            link(dve.scalar_tensor_tensor(biasm[:, :], biash[:, :], cst[0:2, C_N1:C_N1 + 1], bias32[:, :], ALU.mult, ALU.add))
            dve.wait_ge(g_zero, 1)
            for dst, src in ((wkh, wqkvh[:, :]), (wkl, wqkvl[:, :]), (bkr[0:2], biasm[:, :])):
                keys = src[:, D:D + 32].rearrange("p (g d) -> p g d", g=NG)
                dve.tensor_copy(dst[:, :, 1:, :], keys.unsqueeze(2).broadcast_to([src.shape[0], NG, SLOTS - 1, DH]))
            for r in range(R):
                for dst, src in ((wqh, wqkvh[:, :]), (wql, wqkvl[:, :]), (bqr[0:2], biasm[:, :])):
                    heads = src[:, 0:D].rearrange("p (g r d) -> p g r d", g=NG, r=R)[:, :, r, :]
                    dve.tensor_copy(dst[:, r, :, 1:, :], heads.unsqueeze(2).broadcast_to([src.shape[0], NG, SLOTS - 1, DH]))
            dve.memset(bkr[0:1, :, 0, 0:1], 1.0)
            dve.tensor_copy(bvr[0:2, :], biasm[:, D + 32:D + 64])
            dve.tensor_copy(bor[0:2, :], biasm[:, D + 64:]).then_inc(setup, 1)

            dve.wait_ge(a_xh, 1)
            dve.tensor_tensor(xtl[:, W:], ps_x, xth[:, W:], ALU.subtract).then_inc(v_xl, 1)
            dve.wait_ge(e_bias, 1)
            link(dve.tensor_copy(bcol[:, :], b45[:, 512:512 + R + 1]))
            dve.tensor_scalar(bcolm[:, 0:R], bcol[:, 0:R], cst[:, C_SQ:C_SQ + 1], None, ALU.mult)
            dve.tensor_scalar(bcolm[:, R:], bcol[:, R:], cst[:, C_SK:C_SK + 1], None, ALU.mult).then_inc(v_bias, 1)

            def mix_q(b, par, j):
                dve.wait_ge(a_qh, 2 * b + 2 - j)
                for r in (2 * j, 2 * j + 1):
                    cols = slice(r * S, (r + 1) * S)
                    last = dve.scalar_tensor_tensor(qa[:, par, :, r, :], ps_q[:, cols].rearrange("p (a q) -> p a q", a=UB), bcol[:, r:r + 1],
                                                    qh[:, cols].rearrange("p (a q) -> p a q", a=UB), ALU.add, ALU.subtract)
                last.then_inc(v_qa, 1)

            def late_setup():
                for n, at in enumerate((C_MT, C_MT0)):
                    dve.tensor_copy(mask_t[:, n, :, :], cst[:, at:at + W].unsqueeze(1).broadcast_to([P, 8, W]))
                dve.wait_ge(ld_small, 16 * N_SMALL)
                dve.tensor_copy(gh[:, :], g32[:, :])
                link(dve.tensor_copy(woh[:, :, :], wo32[:, :, :]))
                dve.tensor_tensor(wol[:, :, :], wo32[:, :, :], woh[:, :, :], ALU.subtract)
                dve.tensor_tensor(gl[:, :], g32[:, :], gh[:, :], ALU.subtract).then_inc(setup_o, 1)

            def moments_x(lo, hi):
                t, st = rs[:, :, lo:hi], stats[:, lo:hi, :]
                dve.wait_ge(v_st, hi)
                link(dve.tensor_tensor(t[:, 1, :], st[:, :, 1], st[:, :, 4], ALU.subtract))
                link(dve.tensor_tensor(t[:, 0, :], st[:, :, 1], st[:, :, 4], ALU.add))
                link(dve.tensor_tensor(t[:, 2, :], t[:, 1, :], t[:, 1, :], ALU.mult))
                link(dve.tensor_tensor(t[:, 3, :], st[:, :, 2], st[:, :, 5], ALU.add))
                link(dve.scalar_tensor_tensor(t[:, 1, :], t[:, 2, :], D / 4.0, t[:, 3, :], ALU.mult, ALU.add))
                dve.tensor_scalar(t[:, 3, :], t[:, 1, :], 1.0 / D, EPS, ALU.mult, ALU.add).then_inc(v_stats, 1)

            def norm_terms(lo, hi):
                t = rs[:, :, lo:hi]
                dve.wait_ge(a_sq, 1 if lo == 0 else 2)
                link(dve.reciprocal(t[:, 5, :], t[:, 4, :]))
                link(dve.tensor_tensor(t[:, 1, :], t[:, 5, :], t[:, 5, :], ALU.mult))
                link(dve.tensor_tensor(t[:, 2, :], t[:, 1, :], t[:, 3, :], ALU.mult))
                link(dve.tensor_scalar(t[:, 1, :], t[:, 2, :], -0.5, 1.5, ALU.mult, ALU.add))
                link(dve.tensor_tensor(rstd[:, lo:hi], t[:, 5, :], t[:, 1, :], ALU.mult))
                link(dve.scalar_tensor_tensor(nmr[:, lo:hi], t[:, 0, :], -0.5, rstd[:, lo:hi], ALU.mult, ALU.mult))

            def x1_norm(i):
                dve.wait_ge(e_x1, past(i))
                for k in range(TB):
                    blk = bass.ds(i * TB + k, 1)
                    last = dve.tensor_scalar(x1st[:, k, :], xr[:, blk, :].rearrange("p o d -> p (o d)"), rstd[:, blk], nmr[:, blk],
                                             ALU.mult, ALU.add)
                last.then_inc(v_x1, 1)

            def x1_lo(i):
                dve.wait_ge(a_x1h, i + 1)
                dve.tensor_tensor(x1l[:, :], bank[3][:, 512:1024], x1h[:, :], ALU.subtract).then_inc(v_x1l, 1)

            def body(b, par):
                if tail(b):
                    moments_x(0, TB)
                for a in range(UB):
                    t = b * UB + a
                    k = UB * par + a
                    if a == 2 and isinstance(b, int) and b == -1:
                        late_setup()
                    nxt = (a < UB - 1 and has(b, 0)) or (a == UB - 1 and has(b, 1))
                    if nxt:
                        dve.wait_ge(e_scores, t + 2)
                        dve.tensor_reduce(mx[:, (k + 1) % 2, :, :, 0], ps_s[:, :].rearrange("p (r g k) -> p r g k", r=2, g=NG),
                                          AX.X, ALU.max).then_inc(v_mx, 1)
                    if a == 2 and has(b, 1):
                        dve.wait_ge(v_km, b + 2)
                        dve.wait_ge(e_tscores, past(b * UB))
                        for g in range(NG):
                            rows = slice(g * 32, (g + 1) * 32)
                            last = dve.tensor_copy(kbd[rows, 1 - par, g, W:], km[rows, :])
                        last.then_inc(v_kbd, 1)
                    n = b * HB - HB - (a == 0)
                    add = (a == 2 and has(b, -1)) or (a == 0 and has(b, -2))
                    if add:
                        dve.wait_ge(e_op, n + 1)
                        dve.tensor_tensor(xr[:, bass.ds(n, 1), :], ps_m[:, 0:D].unsqueeze(1), xr[:, bass.ds(n, 1), :], ALU.add).then_inc(v_r, 1)
                    if a % 2 == 1 and has(b, -1):
                        dve.wait_ge(a_oth, b * HB - HB + a // 2 + 1)
                        dve.tensor_tensor(otl[:, :], ps_m[:, 0:P], oth[:, :], ALU.subtract).then_inc(v_otl, 1)
                    if a == 2 and has(b, 1):
                        dve.wait_ge(a_vh, b + 2)
                        dve.tensor_tensor(vaug[:, 1 - par, :, :, DH:2 * DH], ps_v.rearrange("p (a g d) -> p a g d", a=UB, g=NG),
                                          vaug[:, 1 - par, :, :, 0:DH], ALU.subtract).then_inc(v_vl, 1)
                    if a % 2 == 1 and has(b, -1 if a == 1 else 0):
                        m = b * HB - (a == 1)
                        dve.wait_ge(e_pv, (m + 1) * 2)
                        o = ps_o.rearrange("p (n c) -> p n c", c=VC)
                        dve.reciprocal(rden[:, :], o[:, :, 2 * DH]).then_inc(v_rden, 1)
                        dve.wait_ge(v_rden, m + 1)
                        dve.wait_ge(g_o, past(m))
                        dve.tensor_tensor(ot2[:, :, :], o[:, :, 0:2 * DH], rden[:, :].unsqueeze(2).broadcast_to([P, 16, 2 * DH]),
                                          ALU.mult).then_inc(v_o, 1)
                    if a == 3 and has(b, 2):
                        dve.wait_ge(a_xh, b + 3)
                        dve.tensor_tensor(xtl[:, W:], ps_x, xth[:, W:], ALU.subtract).then_inc(v_xl, 1)
                    if a == 0 and has(b, 1):
                        dve.wait_ge(a_kh, b + 2)
                        dve.wait_ge(v_kbd, past(b + 1))
                        dve.scalar_tensor_tensor(km[:, :], ps_k, bcol[:, R:], kh[:, :], ALU.add, ALU.subtract).then_inc(v_km, 1)
                    if a < 2 and has(b, 1):
                        mix_q(b + 1, 1 - par, 1 - a)
                    if add:
                        dve.wait_ge(v_r, n + 1)
                    if nxt:
                        dve.wait_ge(e_maxt, t + 2)
                        dve.wait_ge(e_tscores, past(t))
                        nb, na = (par, a + 1) if a < UB - 1 else (1 - par, 0)
                        if na == 0:
                            dve.wait_ge(v_qa, b * 2 + 4)
                        dve.tensor_tensor(qm[:, (k + 1) % 2, :, :], ps_m.rearrange("p (r q) -> p r q", r=R),
                                          qa[:, nb, na, :, :], ALU.add).then_inc(v_qm, 1)
                    if add:
                        dve.bn_stats(stats[:, bass.ds(n, 1), :].rearrange("p o c -> p (o c)"),
                                     xr[:, bass.ds(n, 1), :].rearrange("p o d -> p (o d)")).then_inc(v_st, 1)
                    if a == 0 and tail(b):
                        norm_terms(0, TB)
                        x1_norm(0)
                    if a == 3 and tail(b):
                        x1_lo(0)

            elements(dve, body)
            moments_x(TB, NBLK)
            norm_terms(TB, NBLK)

            dve.wait_ge(g_w, B)
            def groups(i, e):
                j = i * EA + e

                def lo(n):
                    to, rows = (hl, slice(0, P)) if n < HC else (hh, slice(HT, P))
                    src = slice(0, P if n < HC else HT)
                    dve.wait_ge(a_hh, j * (HC + 1) + n + 1)
                    dve.tensor_tensor(to[rows, e % 2, n, :], hf[src, n % 3, :], hh[src, e % 2, n, :], ALU.subtract).then_inc(v_hl, 1)

                for n in range(HC + 1):
                    q = j * (HC + 1) + n
                    rows = slice(0, P if n < HC else HT)
                    w3part = bank[n % 3][:, 512:1024] if n < HC else bank[n % 3][HT:P, 0:512]
                    dve.wait_ge(a_silu, q + 1)
                    dve.wait_ge(a_hh, past(q - 2))
                    if n in LO_POOL:
                        dve.wait_ge(g_hl, j * len(LO_POOL) + LO_POOL.index(n))
                    else:
                        dve.wait_ge(v_hl, past(j * len(LO_DVE) + LO_DVE.index(n) - 1))
                    dve.tensor_tensor(hf[rows, n % 3, :], w3part, sg[rows, n % 3, :], ALU.mult).then_inc(v_hf, 1)
                    if n - 1 in LO_DVE:
                        lo(n - 1)
                lo(HC)

            def combine(i, e):
                dve.wait_ge(e_y, i * EA + e + 1)
                if e == EA - 1:
                    dve.wait_ge(a_out, past(i))
                for k in range(TB):
                    acc = xr[:, bass.ds(i * TB + k, 1), :].rearrange("p o d -> p (o d)")
                    last = dve.scalar_tensor_tensor(yst[:, k, :] if e == EA - 1 else acc, bank[3][:, k * D:(k + 1) * D], cw[:, k, e:e + 1],
                                                    x1st[:, k, :] if e == 0 else acc, ALU.mult, ALU.add)
                last.then_inc(v_y, 1)

            class Chain:
                def __init__(self, s, i, ch, first):
                    self.s, self.i, self.ch, self.n = s, i, ch, first

                def __call__(self, ins):
                    self.n += 1
                    ins.then_inc(self.s, 1)
                    dve.wait_ge(self.s, self.i * self.ch + self.n)

            def gate_ranks(i):
                c = Chain(v_gc, i, NGATE, 0)
                dve.wait_ge(e_gate, i + 1)
                lg = bank[3][:, 512:512 + TB * EA].rearrange("p (k e) -> p k e", k=TB)
                li = ge[:, :, :].unsqueeze(3).broadcast_to([P, TB, EA, EA])
                lj = ge[:, :, :].unsqueeze(2).broadcast_to([P, TB, EA, EA])
                tri = cst[:, C_TRI:C_TRI + EA * EA].rearrange("p (a b) -> p a b", a=EA).unsqueeze(1).broadcast_to([P, TB, EA, EA])
                c(dve.tensor_reduce(gm[:, :], lg, AX.X, ALU.max))
                c(dve.tensor_tensor(ge[:, :, :], lg, gm[:, :].unsqueeze(2).broadcast_to([P, TB, EA]), ALU.subtract))
                dve.tensor_tensor(gt[:, :, :, :], lj, li, ALU.is_gt)
                c(dve.tensor_tensor(eq[:, :, :, :], lj, li, ALU.is_equal))
                c(dve.tensor_tensor(eq[:, :, :, :], eq[:, :, :, :], tri, ALU.mult))
                c(dve.tensor_tensor(gt[:, :, :, :], gt[:, :, :, :], eq[:, :, :, :], ALU.add))
                c(dve.tensor_reduce(rank[:, :, :], gt[:, :, :, :], AX.X, ALU.add))

            def gate_weights(i):
                c = Chain(v_gc, i, NGATE, 6)
                dve.wait_ge(a_ex, i + 1)
                c(dve.scalar_tensor_tensor(cwu[:, :, :], rank[:, :, :], TOPK - 0.5, ex[:, :, :], ALU.is_lt, ALU.mult))
                c(dve.tensor_reduce(gs[:, :], cwu[:, :, :], AX.X, ALU.add))
                c(dve.reciprocal(gr[:, :], gs[:, :]))
                c(dve.tensor_tensor(cw[:, :, :], cwu[:, :, :], gr[:, :].unsqueeze(2).broadcast_to([P, TB, EA]), ALU.mult))
                assert c.n == NGATE

            def moments(i):
                c = Chain(v_fc, i, NFIN, 0)
                dve.wait_ge(v_y, (i + 1) * EA)
                for k in range(TB):
                    last = dve.bn_stats(fst[:, k, :], yst[:, k, :])
                c(last)
                dve.tensor_tensor(fs[:, 1, :], fst[:, :, 1], fst[:, :, 4], ALU.subtract)
                c(dve.tensor_tensor(fs[:, 0, :], fst[:, :, 1], fst[:, :, 4], ALU.add))
                c(dve.tensor_tensor(fs[:, 2, :], fs[:, 1, :], fs[:, 1, :], ALU.mult))
                c(dve.tensor_tensor(fs[:, 5, :], fst[:, :, 2], fst[:, :, 5], ALU.add))
                c(dve.scalar_tensor_tensor(fs[:, 1, :], fs[:, 2, :], D / 4.0, fs[:, 5, :], ALU.mult, ALU.add))
                dve.tensor_scalar(fs[:, 3, :], fs[:, 1, :], 1.0 / D, EPS, ALU.mult, ALU.add).then_inc(v_fv, 1)

            def final(i):
                c = Chain(v_fc, i, NFIN, 5)
                dve.wait_ge(a_fsq, i + 1)
                c(dve.reciprocal(fs[:, 5, :], fs[:, 4, :]))
                c(dve.tensor_tensor(fs[:, 1, :], fs[:, 5, :], fs[:, 5, :], ALU.mult))
                c(dve.tensor_tensor(fs[:, 2, :], fs[:, 1, :], fs[:, 3, :], ALU.mult))
                c(dve.tensor_scalar(fs[:, 1, :], fs[:, 2, :], -0.5, 1.5, ALU.mult, ALU.add))
                c(dve.tensor_tensor(frs[:, :], fs[:, 5, :], fs[:, 1, :], ALU.mult))
                c(dve.scalar_tensor_tensor(fnm[:, :], fs[:, 0, :], -0.5, frs[:, :], ALU.mult, ALU.mult))
                assert c.n == NFIN

            def tile(i):
                inner = not isinstance(i, int)
                groups(i, 0)
                gate_ranks(i)
                if inner or i > 0:
                    combine(i - 1, EA - 1)
                gate_weights(i)
                groups(i, 1)
                if inner or i > 0:
                    moments(i - 1)
                combine(i, 0)
                groups(i, 2)
                if inner or i < NT - 1:
                    x1_norm(i + 1)
                combine(i, 1)
                groups(i, 3)
                if inner or i < NT - 1:
                    x1_lo(i + 1)
                if inner or i > 0:
                    final(i - 1)
                combine(i, 2)

            tile(0)
            with dve.Fori(1, NT - 1) as i:
                tile(i)
            tile(NT - 1)
            combine(NT - 1, EA - 1)
            moments(NT - 1)
            final(NT - 1)


def constants():
    import numpy as np
    c = np.zeros((P, C_ALL), np.float32)
    c[:, C_ID:C_ID + P] = np.eye(P)
    q = np.arange(P)[:, None] % W
    key = np.arange(KW)[None, :]
    seen = (key > q) & (key <= W + q)
    c[:, C_MS:C_MS + KW] = np.where(seen, 0, -1e30)
    c[:, C_MS0:C_MS0 + KW] = np.where(seen & (key >= W), 0, -1e30)
    c[:, C_MT:C_MT + W] = c[0:W, C_MS:C_MS + KW].T
    c[:, C_MT0:C_MT0 + W] = c[0:W, C_MS0:C_MS0 + KW].T
    slot = np.arange(P) % 32 // DH
    c[:, C_SQ] = 1.0 * (slot == 2)
    c[:, C_SK] = 1.0 * (slot == 3)
    c[1, C_N1] = -1.0
    i, j = np.arange(EA)[:, None], np.arange(EA)[None, :]
    c[:, C_TRI:] = (j < i).astype(np.float32).reshape(-1)
    return c


def kernel(L0_attn_x, L0_attn_Wq, L0_attn_bq, L0_attn_Wk, L0_attn_bk, L0_attn_Wv, L0_attn_bv, L0_attn_Wo, L0_attn_bo,
           L0_ffn_gate_w, L0_ffn_w1, L0_ffn_w2, L0_ffn_w3):
    import numpy as np
    import concourse.bacc as bacc
    from concourse.bass_utils import run_bass_kernel_spmd

    nc = bacc.Bacc("TRN2", target_bir_lowering=False, num_devices=1)
    named = {"x": L0_attn_x, "wq": L0_attn_Wq, "bq": L0_attn_bq, "wk": L0_attn_Wk, "bk": L0_attn_bk, "wv": L0_attn_Wv,
             "bv": L0_attn_bv, "wo": L0_attn_Wo, "bo": L0_attn_bo, "gate": L0_ffn_gate_w, "w1": L0_ffn_w1, "w2": L0_ffn_w2,
             "w3": L0_ffn_w3, "const": constants()}
    arrays, args = {}, []
    for name, a in named.items():
        a = np.ascontiguousarray(a)
        arrays[f"in_{name}"] = a
        args.append(nc.dram_tensor(f"in_{name}", a.shape, mybir.dt.from_np(a.dtype), kind="ExternalInput").ap())
    o = nc.dram_tensor("out", (NBLK, P, D), F32, kind="ExternalOutput").ap()
    build(nc, *args, o)
    r = run_bass_kernel_spmd(nc, [arrays], core_ids=[0])
    return r.results[0]["out"].reshape(B, S, D)
```
